# Optimizing a Trainium2 kernel written in Bass

```python
import numpy as np
import jax
import jax.numpy as jnp

def _softmax(x, axis=-1):
    return jax.nn.softmax(x, axis=axis)

def _gelu(x):
    return jax.nn.gelu(x, approximate=True)

def _silu(x):
    return jax.nn.silu(x)

def _sigmoid(x):
    return jax.nn.sigmoid(x)

def _layernorm(x, axis=-1, eps=1e-05):
    m = jnp.mean(x, axis=axis, keepdims=True)
    v = jnp.var(x, axis=axis, keepdims=True)
    return (x - m) / jnp.sqrt(v + eps)

def _scatter_add(tgt, idx, src, axis=0):
    return tgt.at[idx].add(src)

def _segment_sum(src, seg, n):
    return jax.ops.segment_sum(src, seg, n)
kernel_name = 'mk_xattn_ffn_d1_seqx_r4_0aba3b'

def setup_inputs(seed: int=0):
    np.random.seed(seed)
    _w = jnp.asarray

    def _rec_inputs():
        import jax
        import jax.numpy as jnp
        _rk = jax.random.key(seed)
        x = -0.000125 + 0.9999 * jax.random.normal(jax.random.fold_in(_rk, 1), (32, 128, 256), jnp.float32)
        _lenS = 128 - jax.random.randint(jax.random.fold_in(_rk, 7), (32,), 0, max(1, 128 // 4) + 1, jnp.int32)
        _lenS2 = 128 - jax.random.randint(jax.random.fold_in(_rk, 8), (32,), 0, max(1, 128 // 4) + 1, jnp.int32)
        _ctx_1024P = jax.random.normal(jax.random.fold_in(_rk, 11), (32, 16, 256), jnp.float32)
        _ctx_1024c = jax.random.dirichlet(jax.random.fold_in(_rk, 511), 0.3 * jnp.ones((16,), jnp.float32), (32, 128))
        _ctx_1024t = jnp.einsum('bsk,bkd->bsd', _ctx_1024c, _ctx_1024P)
        _ctx_1024t = _ctx_1024t * jax.lax.rsqrt(jnp.mean(jnp.square(_ctx_1024t)) + 1e-12) * 0.953939
        ctx_1024 = -1.52775e-05 + 0.999936 * (_ctx_1024t + 0.3 * jax.random.normal(jax.random.fold_in(_rk, 611), (32, 128, 256), jnp.float32))
        return (x, ctx_1024)
    x, ctx_1024 = _rec_inputs()

    def _L0_xattn_setup():
        import jax, jax.numpy as jnp
        import numpy as np
        NUM_HEADS = 16
        key = jax.random.key(seed)
        ks = jax.random.split(key, 11)
        B, S, DIN, DOUT = (8, 1024, 256, 256)

        def xavier(k, shape):
            fan_in, fan_out = (shape[1], shape[0])
            limit = float(np.sqrt(6.0 / (fan_in + fan_out)))
            return jax.random.uniform(k, shape, jnp.float32, -limit, limit)
        return {'q': jax.random.normal(ks[0], (B, S, DIN), jnp.float32), 'k': jax.random.normal(ks[1], (B, S, DIN), jnp.float32), 'v': jax.random.normal(ks[2], (B, S, DIN), jnp.float32), 'Wq': xavier(ks[3], (DOUT, DIN)), 'bq': jnp.zeros((DOUT,), jnp.float32), 'Wk': xavier(ks[4], (DOUT, DIN)), 'bk': jnp.zeros((DOUT,), jnp.float32), 'Wv': xavier(ks[5], (DOUT, DIN)), 'bv': jnp.zeros((DOUT,), jnp.float32), 'Wd': xavier(ks[6], (DOUT, DOUT)), 'bd': jnp.zeros((DOUT,), jnp.float32)}
    _L0_xattn_all = _L0_xattn_setup()
    _L0_xattn_in = {k: v for k, v in _L0_xattn_all.items() if k in ('Wq', 'bq', 'Wk', 'bk', 'Wv', 'bv', 'Wd', 'bd')}
    del _L0_xattn_all

    def _L0_ffn_setup():
        import jax, jax.numpy as jnp
        import numpy as np
        B, T, E, C, H, G = (2, 512, 8, 256, 512, 16)
        key = jax.random.key(seed)
        ks = jax.random.split(key, 7)
        return {'hidden_states': jax.random.normal(ks[0], (B, T, C), jnp.float32), 'w_red': jax.random.normal(ks[1], (C, G), jnp.float32) * 0.02, 'wg': jax.random.normal(ks[2], (E, G), jnp.float32), 'W1': jax.random.normal(ks[3], (E, C, H), jnp.float32) * 0.02, 'b1': jax.random.normal(ks[4], (E, H), jnp.float32) * 0.02, 'W2': jax.random.normal(ks[5], (E, H, C), jnp.float32) * 0.02, 'b2': jax.random.normal(ks[6], (E, C), jnp.float32) * 0.02}
    _L0_ffn_all = _L0_ffn_setup()
    _L0_ffn_in = {k: v for k, v in _L0_ffn_all.items() if k in ('w_red', 'wg', 'W1', 'b1', 'W2', 'b2')}
    del _L0_ffn_all
    return {'x': x, 'ctx_1024': ctx_1024, 'L0_xattn_Wq': _L0_xattn_in['Wq'], 'L0_xattn_bq': _L0_xattn_in['bq'], 'L0_xattn_Wk': _L0_xattn_in['Wk'], 'L0_xattn_bk': _L0_xattn_in['bk'], 'L0_xattn_Wv': _L0_xattn_in['Wv'], 'L0_xattn_bv': _L0_xattn_in['bv'], 'L0_xattn_Wd': _L0_xattn_in['Wd'], 'L0_xattn_bd': _L0_xattn_in['bd'], 'L0_ffn_w_red': _L0_ffn_in['w_red'], 'L0_ffn_wg': _L0_ffn_in['wg'], 'L0_ffn_W1': _L0_ffn_in['W1'], 'L0_ffn_b1': _L0_ffn_in['b1'], 'L0_ffn_W2': _L0_ffn_in['W2'], 'L0_ffn_b2': _L0_ffn_in['b2']}

def reference(x, ctx_1024, L0_xattn_Wq, L0_xattn_bq, L0_xattn_Wk, L0_xattn_bk, L0_xattn_Wv, L0_xattn_bv, L0_xattn_Wd, L0_xattn_bd, L0_ffn_w_red, L0_ffn_wg, L0_ffn_W1, L0_ffn_b1, L0_ffn_W2, L0_ffn_b2):
    import jax
    import jax.numpy as jnp

    def _L0_xattn_ref(q, k, v, Wq, bq, Wk, bk, Wv, bv, Wd, bd):
        import jax, jax.numpy as jnp
        import numpy as np
        NUM_HEADS = 16
        B = q.shape[0]
        H = NUM_HEADS
        O = Wq.shape[0]
        D = O // H
        query = q @ Wq.T + bq
        key_p = k @ Wk.T + bk
        value = v @ Wv.T + bv
        query = query.reshape(B, -1, H, D)
        key_p = key_p.reshape(B, -1, H, D)
        value = value.reshape(B, -1, H, D)
        logits = jnp.einsum('bsid,bsjd->bsij', query, key_p) / jnp.sqrt(jnp.float32(D))
        attn = jax.nn.softmax(logits, axis=-1)
        out = jnp.einsum('bsij,bsjd->bsid', attn, value)
        out = jnp.transpose(out, (0, 2, 1, 3)).reshape(B, -1, O)
        return out @ Wd.T + bd

    def _L0_ffn_ref(hidden_states, w_red, wg, W1, b1, W2, b2):
        import jax, jax.numpy as jnp
        import numpy as np
        B, T, E, C, H, G = (2, 512, 8, 256, 512, 16)
        b, t, c = hidden_states.shape
        x = hidden_states.reshape(-1, c)
        x_red = x @ w_red
        wg_n = wg / jnp.maximum(jnp.linalg.norm(wg, axis=1, keepdims=True), 0.0001)
        logits = x_red @ wg_n.T
        gates = jax.nn.softmax(logits, axis=1)
        scores = jnp.max(gates, axis=1)
        idx = jnp.argmax(gates, axis=1)
        h = jnp.einsum('nc,ech->neh', x, W1) + b1[None]
        h = jnp.take_along_axis(h, idx[:, None, None], axis=1)[:, 0, :]
        h = jax.nn.gelu(h, approximate=False)
        o = jnp.einsum('nh,ehc->nec', h, W2) + b2[None]
        o = jnp.take_along_axis(o, idx[:, None, None], axis=1)[:, 0, :]
        o = o * scores[:, None]
        return o.reshape(b, t, c)
    x = x + _L0_xattn_ref(_layernorm(x, axis=-1), ctx_1024, ctx_1024, L0_xattn_Wq, L0_xattn_bq, L0_xattn_Wk, L0_xattn_bk, L0_xattn_Wv, L0_xattn_bv, L0_xattn_Wd, L0_xattn_bd)
    x = x + _L0_ffn_ref(_layernorm(x, axis=-1), L0_ffn_w_red, L0_ffn_wg, L0_ffn_W1, L0_ffn_b1, L0_ffn_W2, L0_ffn_b2)
    return x

_drawn_inputs = setup_inputs


def setup_inputs(seed=0):
    import zlib

    import numpy as np

    out = dict(_drawn_inputs(seed))
    spreads = {'L0_xattn_bq': (0.0, 0.1),
     'L0_xattn_bk': (0.0, 0.283),
     'L0_xattn_bv': (0.0, 0.1),
     'L0_xattn_bd': (0.0, 0.1)}
    factors = {'L0_ffn_w_red': 4.191,
     'L0_ffn_wg': 4.185,
     'L0_ffn_W1': 4.169,
     'L0_ffn_b1': 8.0,
     'L0_ffn_W2': 4.045,
     'L0_ffn_b2': 8.0}
    for name, (base, spread) in spreads.items():
        noise = np.random.default_rng([zlib.crc32(name.encode()), seed]).standard_normal(out[name].shape)
        drawn = base * np.exp(spread * noise) if base else spread * noise
        out[name] = jnp.asarray(drawn.astype(out[name].dtype))
    for name, factor in factors.items():
        out[name] = (out[name] * factor).astype(out[name].dtype)
    return out
```

```python
import concourse.bass as bass
from concourse import mybir
from contextlib import ExitStack

P = 128
C = 256
NH = 16
HD = C // NH
NT = 32
NTOK = NT * P
NE = 8
HID = 512
NG = 16
KC = C // P
KH = HID // P
NS = NT + NE - 1
NSP = NS + 1
ROW = 2 * C + 4
BW = 4 * C
EPS = 1e-5
HALF = NH // 2
PVC = 4
PVJ = NH // PVC


class Tile:

    def __init__(self, i, c):
        self.i, self.c, self.par = i, c, c % 2

    def at(self, k=0):
        return self.c + k if self.i is None else self.i * 2 + (self.c + k)

    def turn(self, k=0):
        return self.c // 2 + k if self.i is None else self.i + (self.c // 2 + k)


def build(nc, x, ctx_in, Wq, bq, Wk, bk, Wv, bv, Wd, bd, w_red, wg, W1, b1, W2, b2, out):
    f32, bf16, i32 = mybir.dt.float32, mybir.dt.bfloat16, mybir.dt.int32
    ALU, ACT, AX = mybir.AluOpType, mybir.ActivationFunctionType, mybir.AxisListType.X

    attn_scr = nc.dram_tensor("attn_scr", [NT, NH, P, HD], f32, kind="Internal").ap()
    row_scr = nc.dram_tensor("row_scr", [NTOK, ROW], f32, kind="Internal").ap()
    bias_scr = nc.dram_tensor("bias_scr", [3, BW + NE * (HID + C)], bf16, kind="Internal").ap()
    NB = BW + NE * (HID + C)
    B1O, B2O = BW, BW + NE * HID

    es = ExitStack()
    with es:
        def sb(name, shape, dt=f32):
            return es.enter_context(nc.sbuf_tensor(name, shape, dt))

        sems = {}

        def sem(name):
            if name not in sems:
                sems[name] = es.enter_context(nc.semaphore(name))
            return sems[name]

        w1 = sb("w1", [P, NE * KC * HID])
        w2 = sb("w2", [P, NE * KH * C])
        wT = sb("wT", [P, KC, 4 * C])
        brow = sb("brow", [P, NB], bf16)
        ones = sb("ones", [P, P], bf16)
        ident = sb("ident", [P, P])
        gate = sb("gate", [P, KC, NE])
        half = sb("half", [P, 1])
        xt = [sb(f"xt{k}", [P, C]) for k in range(2)]
        ct = [sb(f"ct{k}", [P, C]) for k in range(2)]
        xr = [sb(f"xr{k}", [P, C]) for k in range(2)]
        ar = [sb(f"ar{k}", [P, C]) for k in range(2)]
        xn = sb("xn", [P, C])
        xcT = sb("xcT", [P, 4, P])
        q = [sb(f"q{k}", [P, C]) for k in range(2)]
        kk = [sb(f"kk{k}", [P, C]) for k in range(2)]
        prod = [sb(f"prod{k}", [P, HALF, C]) for k in range(2)]
        pv = [sb(f"pv{k}", [P, PVJ, C]) for k in range(PVC)]
        lg = sb("lg", [P, NH, NH])
        pr = sb("pr", [P, NH, NH])
        mx = sb("mx", [P, NH])
        sm = sb("sm", [P, NH])
        ao = [sb(f"ao{k}", [P, NH, HD]) for k in range(2)]
        aoT = sb("aoT", [P, KC, P])
        x2T = sb("x2T", [P, KC, P])
        cat = [sb(f"cat{k}", [P, ROW]) for k in range(2)]
        st = [sb(f"st{k}", [P, 6]) for k in range(2)]
        mv = [sb(f"mv{k}", [P, 2]) for k in range(2)]
        ve = [sb(f"ve{k}", [P, 1]) for k in range(2)]
        rs = [sb(f"rs{k}", [P, 1]) for k in range(2)]
        gm = sb("gm", [P, 1])
        ge = sb("ge", [P, NE])
        gs = sb("gs", [P, 1])
        glog = sb("glog", [P, NT, NE])

        def bank(name):
            return es.enter_context(nc.psum_tensor(name, [P, 512], f32))

        bT, bQ, bO, bA, bY, bG = (bank(n) for n in ("bT", "bQ", "bO", "bA", "bY", "bG"))
        bKV = [bank("bKV0"), bank("bKV1")]

        def done(inst, ev, by=1):
            return inst.then_inc(sem(ev), by)

        def need(eng, ev, n):
            if not isinstance(n, int) or n > 0:
                eng.wait_ge(sem(ev), n)

        stage = pv[0][:, :, :].rearrange("p a b -> p (a b)")
        stage2 = pv[1][:, :, :].rearrange("p a b -> p (a b)")
        wst = [(stage if w < 2 else stage2)[:, (w % 2) * 512:(w % 2) * 512 + 512]
               .rearrange("p (a c) -> p a c", a=KC) for w in range(4)]
        NBC = NB // P
        bst = pv[2][:, 0, 0:NBC]
        bres = pv[2][:, 1, 0:NBC]
        bres2 = pv[2][:, 2, 0:NBC]
        bsp = pv[3][:, 0, :].bitcast(bf16)[:, 0:3 * NBC].rearrange("p (k f) -> p k f", k=3)
        wrp = pv[3][:, 1:3, 0:P]
        wgb = pv[3][:, 3, 0:NE * NG]
        wgs = pv[3][:, 3, NE * NG:2 * NE * NG]
        wgT = q[0][:, 0:NE]
        wrT = q[0][:, NE:NE]
        wrT = kk[0][:, :].rearrange("p (a c) -> p a c", a=KC)
        nrm = q[1][:, 0:NE]
        nr2 = q[1][:, NE:2 * NE]
        nr3 = q[1][:, 2 * NE:3 * NE]

        pieces = [(b, k * 2, 2, k * C) for k, b in enumerate((bq, bk, bv, bd))]
        pieces += [(b1.rearrange("e h -> (e h)"), 8, NE * HID // P, B1O),
                   (b2.rearrange("e h -> (e h)"), 8 + NE * HID // P, NE * C // P, B2O)]

        with nc.Block() as block:
            @block.sync
            def _(eng):
                for w, src in enumerate((Wq, Wk, Wv, Wd)):
                    done(eng.dma_start(wst[w], src.rearrange("(a p) c -> p a c", p=P)), "ld_w", 16)
                for src, o, n, _ in pieces:
                    done(eng.dma_start(bst[:, o:o + n], src.rearrange("(p f) -> p f", p=P)), "ld_b", 16)
                need(eng, "pad0", 1)
                done(eng.dma_start(wrp[:, :, 0:NG], w_red.rearrange("(a p) g -> p a g", p=P)), "ld_g", 16)
                done(eng.dma_start(wgb, wg.rearrange("e g -> (e g)").rearrange("(o n) -> o n", o=1)
                                   .broadcast_to((P, NE * NG))), "ld_g", 16)
                with nc.allow_non_contiguous_dma("wg transposed, 128 elements"):
                    done(eng.dma_start(wgT[0:NG, :], wg.rearrange("e g -> g e")), "ld_g", 16)
                need(eng, "bsplit", 1)
                for _, o, n, off in pieces:
                    done(eng.dma_start(bias_scr[:, off:off + n * P].rearrange("k (p f) -> p k f", p=P),
                                       bsp[:, :, o:o + n]), "st_b", 16)
                need(eng, "st_b", 16 * len(pieces))
                need(eng, "brow0", 1)
                done(eng.dma_start(brow[0:3, :], bias_scr), "ld_br", 16)
                need(eng, "ld_br", 16)

            @block.gpsimd
            def _(eng):
                done(eng.memset(ident[:, :], 0.0), "c_id")
                need(eng, "c_id", 1)
                done(eng.affine_select(out=ident[:, :], in_=ident[:, :], compare_op=ALU.not_equal, fill=1.0,
                                       base=0, pattern=[[-1, P]], channel_multiplier=1), "ident")
                done(eng.memset(wrp, 0.0), "pad0")
                eng.memset(ones[:, :], 1.0)
                eng.memset(half[:, :], -0.5)
                done(eng.memset(brow[:, :], 0.0), "brow0")

            @block.vector
            def _(eng):
                need(eng, "ld_b", 16 * len(pieces))
                done(eng.tensor_copy(bsp[:, 0, :], bst), "v0")
                need(eng, "v0", 1)
                done(eng.tensor_tensor(bres, bst, bsp[:, 0, :], ALU.subtract), "v0")
                need(eng, "v0", 2)
                done(eng.tensor_copy(bsp[:, 1, :], bres), "v0")
                need(eng, "v0", 3)
                done(eng.tensor_tensor(bres2, bres, bsp[:, 1, :], ALU.subtract), "v0")
                need(eng, "v0", 4)
                done(eng.tensor_copy(bsp[:, 2, :], bres2), "bsplit")
                need(eng, "ld_g", 48)
                done(eng.tensor_tensor(wgs, wgb, wgb, ALU.mult), "v0")
                need(eng, "v0", 5)
                done(eng.tensor_reduce(nrm, wgs.rearrange("p (e g) -> p e g", e=NE), AX, ALU.add), "nrm")
                need(eng, "nsq", 1)
                done(eng.tensor_scalar(nr3, nr2, 1e-4, None, ALU.max), "v0")
                need(eng, "v0", 6)
                done(eng.reciprocal(nrm, nr3), "v0")
                for w in range(4):
                    b = (bT, bQ, bO, bA)[w]
                    need(eng, "wtr", w + 1)
                    done(eng.tensor_copy(wT[:, :, w * C:(w + 1) * C],
                                         b[:, :].rearrange("p (a c) -> p a c", a=KC)), "v0")
                need(eng, "wrt", 1)
                done(eng.tensor_copy(wrT[:, :, :], bY[:, 0:C].rearrange("p (a c) -> p a c", a=KC)), "wrTs")
                need(eng, "gmm", 1)
                need(eng, "v0", 7)
                done(eng.tensor_tensor(gate[:, :, :], bG[:, 0:KC * NE].rearrange("p (a e) -> p a e", a=KC),
                                       nrm.unsqueeze(1).broadcast_to((P, KC, NE)), ALU.mult), "v0")

            @block.scalar
            def _(eng):
                for s_, d_ in ((W1, w1), (W2, w2)):
                    k_ = KC if d_ is w1 else KH
                    dv = d_[:, :].rearrange("p (e k n) -> p e k n", e=NE, k=k_)
                    for e in range(NE):
                        done(eng.dma_start(dv[:, e, :, :], s_[e].rearrange("(k p) n -> p k n", p=P)),
                             "ld_moe", 16)
                need(eng, "nrm", 1)
                done(eng.activation(nr2, nrm, ACT.Sqrt), "nsq")

            @block.tensor
            def _(eng):
                need(eng, "ident", 1)
                need(eng, "ld_w", 64)
                for w in range(4):
                    b = (bT, bQ, bO, bA)[w]
                    for a in range(KC):
                        for c in range(KC):
                            i_ = eng.transpose(b[:, c * C + a * P:c * C + (a + 1) * P],
                                               wst[w][:, a, c * P:(c + 1) * P], ident[:, :])
                    done(i_, "wtr")
                need(eng, "ld_g", 48)
                for a in range(KC):
                    i_ = eng.transpose(bY[:, a * P:(a + 1) * P], wrp[:, a, :], ident[:, :])
                done(i_, "wrt")
                need(eng, "wrTs", 1)
                for a in range(KC):
                    i_ = eng.matmul(bG[:, a * NE:(a + 1) * NE], wrT[0:NG, a, :], wgT[0:NG, :],
                                    start=True, stop=True)
                done(i_, "gmm")

        FIRST, LAGS = 6, 3

        def steps(eng, body, total, first, lags):
            def step(i, c):
                def on(lag):
                    n = Tile(i, c - lag)
                    return n if i is not None or 0 <= c - lag < total else None
                body(on)
            last = first + (total - first) // 2 * 2
            for c in range(first):
                step(None, c)
            with eng.Fori(0, (last - first) // 2) as i:
                for u in range(2):
                    step(i, first + u)
            for c in range(last, total + lags):
                step(None, c)

        def load_in(eng, n):
            need(eng, "xn", n.at(-1))
            done(eng.dma_start(xt[n.par][:, :], x[n.at()]), f"ld_x{n.par}", 16)
            need(eng, "tr_in", n.at(-1))
            done(eng.dma_start(ct[n.par][:, :], ctx_in[n.at()]), f"ld_c{n.par}", 16)

        with nc.Block() as block:
            @block.sync
            def _(eng):
                def body(on):
                    a, b, c, d = (on(k) for k in range(4))
                    if a:
                        load_in(eng, a)
                    if c:
                        need(eng, "x2", c.at(-1))
                        done(eng.dma_start(xr[c.par][:, :], x[c.at()]), f"ld_xr{c.par}", 16)
                    if d:
                        need(eng, "score", d.at(1))
                        done(eng.dma_start(row_scr[bass.ds(d.at() * P, P), :] if not isinstance(d.at(), int)
                                           else row_scr[d.at() * P:(d.at() + 1) * P, :], cat[d.par][:, :]),
                             f"st_r{d.par}", 16)
                    if b:
                        need(eng, "onorm", b.at(1))
                        done(eng.dma_start(attn_scr[b.at()].rearrange("i t d -> t i d"), ao[b.par][:, :, :]),
                             f"st_a{b.par}", 16)
                        need(eng, f"st_a{b.par}", b.turn(1) * 16)
                        need(eng, "tr_a", b.at(-1))
                        done(eng.dma_start(ar[b.par][:, :], attn_scr[b.at()].rearrange("i (a b) d -> (i a) (b d)", b=NH)),
                             f"ld_a{b.par}", 16)
                steps(eng, body, NT, FIRST, LAGS)
                for k in range(2):
                    need(eng, f"st_r{k}", NT // 2 * 16)

            @block.gpsimd
            def _(eng):
                def body(on):
                    a, b, c, d = (on(k) for k in range(4))
                    for h in range(2):
                        if b:
                            if h == 0:
                                need(eng, "kcp", b.at(1))
                            need(eng, f"qkred{h}", b.at(0))
                            i_ = eng.tensor_tensor(
                                prod[h][:, :, :].rearrange("p i (j d) -> p i j d", j=NH),
                                q[b.par][:, h * HALF * HD:(h + 1) * HALF * HD].rearrange("p (i d) -> p i d", d=HD)
                                .unsqueeze(2).broadcast_to((P, HALF, NH, HD)),
                                kk[b.par][:, :].rearrange("p (j d) -> p j d", d=HD)
                                .unsqueeze(1).broadcast_to((P, HALF, NH, HD)), ALU.mult)
                            done(i_, f"qk{h}")
                    for n, w in ((a, 0), (c, 1)):
                        if n:
                            need(eng, f"ve{w}", n.at(1))
                            need(eng, "xn" if w == 0 else "x2n", n.at(0))
                            done(eng.tensor_tensor(rs[w][:, :], ve[w][:, :], half[:, :], ALU.pow), f"rs{w}")
                steps(eng, body, NT, FIRST, LAGS)

            def stats(eng, w, src):
                done(eng.bn_stats(st[w][:, :], src), f"st{w}")
                return src

            @block.vector
            def _(eng):
                def body(on):
                    a, b, c, d = (on(k) for k in range(4))

                    def qk_sum(h):
                        need(eng, f"qk{h}", b.at(1))
                        done(eng.tensor_reduce(lg[:, h * HALF:(h + 1) * HALF, :],
                                               prod[h][:, :, :].rearrange("p i (j d) -> p i j d", j=NH),
                                               AX, ALU.add), f"qkred{h}")

                    if c:
                        need(eng, f"ld_xr{c.par}", c.turn(1) * 16)
                        need(eng, "wd", c.at(1))
                        need(eng, f"st_r{c.par}", c.turn(0) * 16)
                        done(eng.tensor_tensor(cat[c.par][:, C:2 * C], bY[:, 0:C], xr[c.par][:, :], ALU.add), "x2")
                    if a:
                        need(eng, f"ld_x{a.par}", a.turn(1) * 16)
                        done(eng.bn_stats(st[0][:, :], xt[a.par][:, :]), "st0")
                    if c:
                        need(eng, "x2", c.at(1))
                        done(eng.bn_stats(st[1][:, :], cat[c.par][:, C:2 * C]), "st1")
                    if a:
                        need(eng, "st0", a.at(1))
                    if c:
                        need(eng, "st1", c.at(1))
                    if b:
                        qk_sum(0)
                    if a:
                        done(eng.bn_aggr(mv[0][:, :], st[0][:, :]), "mv0")
                    if c:
                        done(eng.bn_aggr(mv[1][:, :], st[1][:, :]), "mv1")
                    if a:
                        need(eng, "mv0", a.at(1))
                        need(eng, "rs0", a.at(0))
                        done(eng.tensor_scalar(ve[0][:, :], mv[0][:, 1:2], EPS, None, ALU.add), "ve0")
                    if c:
                        need(eng, "mv1", c.at(1))
                        need(eng, "rs1", c.at(0))
                        done(eng.tensor_scalar(ve[1][:, :], mv[1][:, 1:2], EPS, None, ALU.add), "ve1")
                    if b:
                        qk_sum(1)
                        need(eng, "qkred1", b.at(1))
                        done(eng.tensor_reduce(mx[:, :], lg[:, :, :], AX, ALU.max), "mx")
                    if a:
                        need(eng, "rs0", a.at(1))
                        need(eng, "tr_in", a.at(0))
                        done(eng.tensor_scalar(xn[:, :], xt[a.par][:, :], mv[0][:, 0:1], rs[0][:, :],
                                               ALU.subtract, ALU.mult), "xn")
                    if b:
                        need(eng, "mx", b.at(1))
                        done(eng.tensor_tensor(lg[:, :, :], lg[:, :, :],
                                               mx[:, :].unsqueeze(2).broadcast_to((P, NH, NH)),
                                               ALU.subtract), "lsub")
                    if c:
                        need(eng, "rs1", c.at(1))
                        done(eng.tensor_scalar(cat[c.par][:, 0:C], cat[c.par][:, C:2 * C], mv[1][:, 0:1],
                                               rs[1][:, :], ALU.subtract, ALU.mult), "x2n")
                    if b:
                        need(eng, "exp", b.at(1))
                        done(eng.tensor_reduce(sm[:, :], pr[:, :, :], AX, ALU.add), "sm")
                    for g in range(PVC):
                        if b:
                            need(eng, f"pvm{g}", b.at(0))
                            v = bKV[b.par][:, C + g * PVJ * HD:C + (g + 1) * PVJ * HD]
                            i_ = eng.tensor_tensor(
                                pv[g][:, :, :].rearrange("p j (i d) -> p j i d", i=NH),
                                v.rearrange("p (j d) -> p j d", d=HD).unsqueeze(2).broadcast_to((P, PVJ, NH, HD)),
                                pr[:, :, g * PVJ:(g + 1) * PVJ].rearrange("p i j -> p j i")
                                .unsqueeze(3).broadcast_to((P, PVJ, NH, HD)), ALU.mult)
                            done(i_, f"pv{g}")
                        if b and g == 1:
                            need(eng, "sm", b.at(1))
                            done(eng.reciprocal(mx[:, :], sm[:, :]), "rsm")
                    if d:
                        need(eng, "glg", d.at(1))
                        done(eng.tensor_reduce(gm[:, :], bG[:, C:C + NE], AX, ALU.max), "gm")
                        need(eng, "gm", d.at(1))
                        done(eng.tensor_scalar(glog[:, d.at(), :], bG[:, C:C + NE], gm[:, :], None,
                                               ALU.subtract), "gsub")
                    if b:
                        need(eng, f"pvm{PVC - 1}", b.at(1))
                        need(eng, f"st_a{b.par}", b.turn(0) * 16)
                        need(eng, "rsm", b.at(1))
                        done(eng.tensor_tensor(ao[b.par][:, :, :], bO[:, 0:C].rearrange("p (i d) -> p i d", i=NH),
                                               mx[:, :].unsqueeze(2).broadcast_to((P, NH, HD)), ALU.mult), "onorm")
                    if d:
                        need(eng, "gexp", d.at(1))
                        done(eng.reciprocal(cat[d.par][:, 2 * C:2 * C + 1], gs[:, :]), "score")
                for k in range(2):
                    eng.memset(cat[k][:, 2 * C:ROW], 0.0)
                steps(eng, body, NT, FIRST, LAGS)

            @block.scalar
            def _(eng):
                def body(on):
                    a, b, c, d = (on(k) for k in range(4))
                    if c:
                        need(eng, "tr_a", c.at(1))
                        need(eng, "wd", c.at(0))
                        done(eng.activation(aoT[:, :, :], bA[:, 0:C].rearrange("p (a c) -> p a c", a=KC),
                                            ACT.Copy), "aoT")
                    if b:
                        need(eng, "lsub", b.at(1))
                        need(eng, f"pv{PVC - 1}", b.at(0))
                        done(eng.activation(pr[:, :, :], lg[:, :, :], ACT.Exp, scale=HD ** -0.5), "exp")
                    if d:
                        need(eng, "tr_g", d.at(1))
                        need(eng, "glg", d.at(0))
                        done(eng.activation(x2T[:, :, :], bG[:, 0:C].rearrange("p (a c) -> p a c", a=KC),
                                            ACT.Copy), "x2T")
                    if a:
                        need(eng, "tr_in", a.at(1))
                        need(eng, "kv", a.at(0))
                        done(eng.activation(xcT[:, :, :], bT[:, :].rearrange("p (a c) -> p a c", a=4),
                                            ACT.Copy), "xcT")
                        need(eng, "kv", a.at(1))
                        need(eng, "qk1", a.at(-1))
                        done(eng.activation(q[a.par][:, :], bQ[:, 0:C], ACT.Copy), "qcp")
                        done(eng.activation(kk[a.par][:, :], bKV[a.par][:, 0:C], ACT.Copy), "kcp")
                    if d:
                        need(eng, "gsub", d.at(1))
                        done(eng.activation(ge[:, :], glog[:, d.at(), :], ACT.Exp, accum_out=gs[:, :]), "gexp")
                steps(eng, body, NT, FIRST, LAGS)
                need(eng, "ld_moe", 16 * 2 * NE)

            @block.tensor
            def _(eng):
                def bias(dst, off, n, start=False, stop=True):
                    return eng.matmul(dst, ones[:, :], brow[:, off:off + n], start=start, stop=stop)

                def body(on):
                    a, b, c, d = (on(k) for k in range(4))
                    if c:
                        need(eng, f"ld_a{c.par}", c.turn(1) * 16)
                        need(eng, "aoT", c.at(0))
                        for k in range(KC):
                            i_ = eng.transpose(bA[:, k * P:(k + 1) * P], ar[c.par][:, k * P:(k + 1) * P],
                                               ident[:, :])
                        done(i_, "tr_a")
                    if a:
                        need(eng, f"ld_c{a.par}", a.turn(1) * 16)
                        need(eng, "xcT", a.at(0))
                        for k in range(KC):
                            eng.transpose(bT[:, (KC + k) * P:(KC + k + 1) * P], ct[a.par][:, k * P:(k + 1) * P],
                                          ident[:, :])
                    if c:
                        need(eng, "aoT", c.at(1))
                        need(eng, "x2", c.at(0))
                        bias(bY[:, 0:C], 3 * C, C, start=True, stop=False)
                        for k in range(KC):
                            i_ = eng.matmul(bY[:, 0:C], aoT[:, k, :], wT[:, k, 3 * C:4 * C],
                                            start=False, stop=(k == KC - 1))
                        done(i_, "wd")
                    if d:
                        need(eng, "x2n", d.at(1))
                        need(eng, "gsub", d.at(0))
                        for k in range(KC):
                            i_ = eng.transpose(bG[:, k * P:(k + 1) * P], cat[d.par][:, k * P:(k + 1) * P],
                                               ident[:, :])
                        done(i_, "tr_g")
                    if a:
                        need(eng, "xn", a.at(1))
                        for k in range(KC):
                            i_ = eng.transpose(bT[:, k * P:(k + 1) * P], xn[:, k * P:(k + 1) * P], ident[:, :])
                        done(i_, "tr_in")
                    if d:
                        need(eng, "x2T", d.at(1))
                        for k in range(KC):
                            i_ = eng.matmul(bG[:, C:C + NE], x2T[:, k, :], gate[:, k, :],
                                            start=(k == 0), stop=(k == KC - 1))
                        done(i_, "glg")
                    if a:
                        need(eng, "xcT", a.at(1))
                        need(eng, "qcp", a.at(0))
                        bias(bQ[:, 0:C], 0, C, start=True, stop=False)
                        for k in range(KC):
                            eng.matmul(bQ[:, 0:C], xcT[:, k, :], wT[:, k, 0:C], start=False, stop=(k == KC - 1))
                        need(eng, f"pv{PVC - 1}", a.at(-1))
                        need(eng, "kcp", a.at(-1))
                        bias(bKV[a.par][:, :], C, 2 * C, start=True, stop=False)
                        for k in range(KC):
                            i_ = eng.matmul(bKV[a.par][:, :], xcT[:, KC + k, :], wT[:, k, C:3 * C],
                                            start=False, stop=(k == KC - 1))
                        done(i_, "kv")
                    if b:
                        need(eng, "onorm", b.at(0))
                        for g in range(PVC):
                            need(eng, f"pv{g}", b.at(1))
                            for j in range(PVJ):
                                i_ = eng.matmul(bO[:, 0:C], ident[:, :], pv[g][:, j, :],
                                                start=(g == 0 and j == 0), stop=(g == PVC - 1 and j == PVJ - 1))
                            done(i_, f"pvm{g}")
                steps(eng, body, NT, FIRST, LAGS)

        def fl(t):
            return t[:, :, :].rearrange("p a b -> p (a b)")

        r0, r1 = fl(prod[0]), fl(prod[1])
        oh = sb("oh", [P, NT, NE], bf16)
        tri = sb("tri", [P, P], bf16)
        idg = sb("idg", [P, NSP], i32)
        ids = sb("ids", [P, NSP], i32)
        texp = sb("texp", [P, NSP], i32)
        io_e = r0[:, 0:256].rearrange("p (n e) -> p n e", e=NE)
        io_m = r0[:, 256:512].rearrange("p (e m) -> p e m", e=NE)
        io_r = r0[:, 512:640]
        io_k = r0[:, 640:640 + NSP]
        seg = r0[:, 704:960].rearrange("p (e n) -> p e n", e=NE)
        one8 = r0[:, 960:960 + NE]
        pid = r0[:, 970:971]
        io_n = r0[:, 992:992 + NT]
        key = r0[:, 1024:1280].rearrange("p (n e) -> p n e", e=NE)
        top = r0[:, 1280:1280 + NT]
        tot = r0[:, 1312:1568].rearrange("p (e n) -> p e n", e=NE)
        inc = r0[:, 1568:1824].rearrange("p (e n) -> p e n", e=NE)
        til = r0[:, 1824:1824 + NE]
        tinc = r0[:, 1840:1840 + NE]
        texc = r0[:, 1856:1856 + NE]
        gtm = r1[:, 0:256].rearrange("p (e m) -> p e m", e=NE)
        exc = r1[:, 256:512].rearrange("p (e n) -> p e n", e=NE)
        slot = r1[:, 512:768].rearrange("p (n e) -> p n e", e=NE)
        pos = r1[:, 768:800]
        posr = r1[:, 800:832]
        posk = r1[:, 832:864]
        pint = r1[:, 864:896].bitcast(i32)
        pir = r1[:, 896:928].bitcast(i32)
        pik = r1[:, 928:960].bitcast(i32)
        tcmp = r1[:, 960:960 + NSP * NE].rearrange("p (k e) -> p k e", e=NE)
        tsum = r1[:, 1280:1280 + NSP]
        tmin = r1[:, 1320:1320 + NSP]
        inv = r1[:, 1360:1360 + NSP]
        emp = r1[:, 1400:1400 + NSP]
        inv2 = r1[:, 1440:1440 + NSP]
        selr = [pv[k][:, :, :].rearrange("p a b -> p (a b)").bitcast(bf16)
                .rearrange("p (n r) -> p n r", r=P) for k in range(2)]
        selk = [pv[2 + k][:, :, :].rearrange("p a b -> p (a b)").bitcast(bf16)[:, 0:16 * 3 * NSP]
                .rearrange("p (n w k) -> p n w k", w=3, k=NSP) for k in range(2)]

        with nc.Block() as block:
            @block.gpsimd
            def _(eng):
                eng.iota(io_e, [[0, NT], [-1, NE]], base=NE, channel_multiplier=0, allow_small_or_imprecise_dtypes=True)
                eng.iota(io_m, [[0, NE], [P, NT]], base=0, channel_multiplier=0, allow_small_or_imprecise_dtypes=True)
                eng.iota(io_r, [[1, P]], base=0, channel_multiplier=0, allow_small_or_imprecise_dtypes=True)
                eng.iota(io_k, [[1, NSP]], base=0, channel_multiplier=0, allow_small_or_imprecise_dtypes=True)
                eng.iota(io_n, [[1, NT]], base=0, channel_multiplier=0, allow_small_or_imprecise_dtypes=True)
                eng.iota(pid, [[0, 1]], base=0, channel_multiplier=1, allow_small_or_imprecise_dtypes=True)
                eng.memset(one8, 1.0)
                eng.memset(seg, 1.0)
                done(eng.memset(tri[:, :], 1.0), "rc0")
                need(eng, "rc0", 1)
                done(eng.memset(seg[:, :, 0:1], 0.0), "rc1")
                done(eng.affine_select(out=tri[:, :], in_=tri[:, :], compare_op=ALU.is_gt, fill=0.0, base=0,
                                       pattern=[[1, P]], channel_multiplier=-1), "rconst")

            @block.vector
            def _(eng):
                steps_ = [0]

                def then(i_):
                    steps_[0] += 1
                    done(i_, "rv")
                    need(eng, "rv", steps_[0])

                need(eng, "rconst", 1)
                then(eng.scalar_tensor_tensor(key, glog[:, :, :], 0.0, io_e, ALU.is_ge, ALU.mult))
                then(eng.tensor_reduce(top, key, AX, ALU.max))
                done(eng.tensor_tensor(oh[:, :, :], key, top.unsqueeze(2).broadcast_to((P, NT, NE)),
                                       ALU.is_equal), "oh")
                need(eng, "cnt", 1)
                then(eng.tensor_copy(tot, bT[:, 0:NT * NE].rearrange("p (n e) -> p e n", e=NE)))
                then(eng.tensor_tensor_scan(inc.rearrange("p e n -> p (e n)"), seg.rearrange("p e n -> p (e n)"),
                                            tot.rearrange("p e n -> p (e n)"), 0.0, ALU.mult, ALU.add))
                then(eng.tensor_tensor(gtm, inc[:, :, NT - 1:NT].broadcast_to((P, NE, NT)), io_m, ALU.is_gt))
                then(eng.tensor_reduce(til, gtm, AX, ALU.add))
                then(eng.tensor_tensor_scan(tinc, one8, til, 0.0, ALU.mult, ALU.add))
                then(eng.tensor_tensor(tcmp, tinc.unsqueeze(1).broadcast_to((P, NSP, NE)),
                                       io_k.unsqueeze(2).broadcast_to((P, NSP, NE)), ALU.is_le))
                then(eng.tensor_reduce(tsum, tcmp, AX, ALU.add))
                then(eng.tensor_scalar(tmin, tsum, float(NE - 1), None, ALU.min))
                done(eng.tensor_copy(texp[:, :], tmin), "texp")
                then(eng.tensor_tensor(texc, tinc, til, ALU.subtract))
                then(eng.tensor_tensor(exc, inc, tot, ALU.subtract))
                then(eng.scalar_tensor_tensor(inc, texc.unsqueeze(2).broadcast_to((P, NE, NT)), float(P), exc,
                                              ALU.mult, ALU.add))
                then(eng.tensor_tensor(slot, bQ[:, 0:NT * NE].rearrange("p (n e) -> p n e", e=NE),
                                       inc.rearrange("p e n -> p n e"), ALU.add))
                then(eng.tensor_tensor(slot, slot, oh[:, :, :], ALU.mult))
                then(eng.tensor_reduce(pos, slot, AX, ALU.add))
                then(eng.tensor_copy(pint, pos))
                then(eng.tensor_scalar(pir, pint, P - 1, None, ALU.bitwise_and))
                then(eng.tensor_scalar(pik, pint, P.bit_length() - 1, None, ALU.logical_shift_right))
                then(eng.tensor_copy(posr, pir))
                then(eng.tensor_copy(posk, pik))
                for k in range(2):
                    n = slice(k * 16, k * 16 + 16)
                    done(eng.tensor_tensor(selr[k], io_r.unsqueeze(1).broadcast_to((P, 16, P)),
                                           posr[:, n].unsqueeze(2).broadcast_to((P, 16, P)), ALU.is_equal), "selr")
                    then(eng.tensor_tensor(selk[k][:, :, 0, :], io_k.unsqueeze(1).broadcast_to((P, 16, NSP)),
                                           posk[:, n].unsqueeze(2).broadcast_to((P, 16, NSP)), ALU.is_equal))
                    done(eng.tensor_scalar(selk[k][:, :, 1, :], selk[k][:, :, 0, :], pid, None, ALU.mult), "selp")
                    done(eng.tensor_tensor(selk[k][:, :, 2, :], selk[k][:, :, 0, :],
                                           io_n[:, n].unsqueeze(2).broadcast_to((P, 16, NSP)), ALU.mult), "selk")
                need(eng, "invmm", 1)
                then(eng.tensor_copy(inv2, bO[:, NSP:2 * NSP]))
                then(eng.scalar_tensor_tensor(inv, bO[:, 2 * NSP:3 * NSP], float(P), inv2, ALU.mult, ALU.add))
                then(eng.tensor_scalar(emp, bO[:, 0:NSP], -float(NTOK), float(NTOK), ALU.mult, ALU.add))
                then(eng.tensor_tensor(emp, emp, inv, ALU.add))
                done(eng.tensor_copy(idg[:, :], inv), "inv")
                done(eng.tensor_copy(ids[:, :], emp), "inv")

            @block.tensor
            def _(eng):
                need(eng, "oh", 1)
                need(eng, "rconst", 1)
                ohf = oh[:, :, :].rearrange("p n e -> p (n e)")
                eng.matmul(bQ[:, 0:NT * NE], tri[:, :], ohf, start=True, stop=True)
                done(eng.matmul(bT[:, 0:NT * NE], ones[:, :], ohf, start=True, stop=True), "cnt")
                for n in range(NT):
                    k = n // 16
                    if n % 16 == 0:
                        need(eng, "selk", k + 1)
                    i_ = eng.matmul(bO[:, 0:3 * NSP], selr[k][:, n % 16, :],
                                    selk[k][:, n % 16, :, :].rearrange("p w k -> p (w k)"),
                                    start=(n == 0), stop=(n == NT - 1))
                done(i_, "invmm")

        ig = [sb(f"ig{k}", [P, 1], i32) for k in range(2)]
        isc = [sb(f"isc{k}", [P, 1], i32) for k in range(2)]
        gr = [sb(f"gr{k}", [P, ROW]) for k in range(2)]
        gT = sb("gT", [P, KC, P])
        hs = [sb(f"hs{k}", [P, HID]) for k in range(2)]
        hT = sb("hT", [P, KH, P])
        yo = [sb(f"yo{k}", [P, C]) for k in range(2)]
        held = sb("held", [P, 1])
        bH = [bO, bA]
        bHT = bKV

        with nc.Block() as block:
            @block.gpsimd
            def _(eng):
                def hold(eng):
                    eng.tensor_tensor(held[:, :], half[:, :], half[:, :], ALU.add)

                need(eng, "inv", 2)

                def body(on):
                    a, c = on(0), on(2)
                    if a:
                        at = eng.snap(a.at())
                        need(eng, f"gat{a.par}", a.turn(0) * 16)
                        done(eng.tensor_copy(ig[a.par][:, :], idg[:, bass.ds(at, 1)]), "ig")
                        need(eng, "ig", a.at(1))
                        need(eng, "yo", a.at(-1))
                        hold(eng)
                        done(eng.indirect_dma_start(gr[a.par][:, :], None, row_scr,
                                                    bass.IndirectOffsetOnAxis(ap=ig[a.par][:, :], axis=0)),
                             f"gat{a.par}", 16)
                    if c:
                        at = eng.snap(c.at())
                        need(eng, f"sca{c.par}", c.turn(0) * 16)
                        done(eng.tensor_copy(isc[c.par][:, :], ids[:, bass.ds(at, 1)]), "isc")
                        need(eng, "isc", c.at(1))
                        need(eng, "yo", c.at(1))
                        hold(eng)
                        done(eng.indirect_dma_start(out, bass.IndirectOffsetOnAxis(ap=isc[c.par][:, :], axis=0),
                                                    yo[c.par][:, :], None, bounds_check=NTOK - 1,
                                                    oob_is_err=False), f"sca{c.par}", 16)
                steps(eng, body, NS, 4, 2)
                need(eng, "sca0", (NS + 1) // 2 * 16)
                need(eng, "sca1", NS // 2 * 16)

            @block.tensor
            def _(eng):
                def body(on):
                    a, b = on(0), on(1)
                    if a:
                        e = eng.value_load(texp[0:1, bass.ds(a.at(), 1)], min_val=0, max_val=NE - 1)
                        need(eng, f"gat{a.par}", a.turn(1) * 16)
                        need(eng, "gT", a.at(0))
                        for k in range(KC):
                            i_ = eng.transpose(bT[:, k * P:(k + 1) * P], gr[a.par][:, k * P:(k + 1) * P],
                                               ident[:, :])
                        done(i_, "gtr")
                        need(eng, "gel", a.at(-1))
                        eng.matmul(bH[a.par][:, :], ones[:, :], brow[:, bass.ds(e * HID + B1O, HID)],
                                   start=True, stop=False)
                        need(eng, "gT", a.at(1))
                        for k in range(KC):
                            i_ = eng.matmul(bH[a.par][:, :], gT[:, k, :],
                                            w1[:, bass.ds(e * (KC * HID) + k * HID, HID)],
                                            start=False, stop=(k == KC - 1))
                        done(i_, "up")
                    if b:
                        e = eng.value_load(texp[0:1, bass.ds(b.at(), 1)], min_val=0, max_val=NE - 1)
                        need(eng, "gel", b.at(1))
                        need(eng, "hT", b.at(-1))
                        for k in range(KH):
                            i_ = eng.transpose(bHT[b.par][:, k * P:(k + 1) * P],
                                               hs[b.par][:, k * P:(k + 1) * P], ident[:, :])
                        done(i_, "htr")
                        need(eng, "yo", b.at(0))
                        eng.matmul(bY[:, 0:C], ones[:, :], brow[:, bass.ds(e * C + B2O, C)],
                                   start=True, stop=False)
                        need(eng, "hT", b.at(1))
                        for k in range(KH):
                            i_ = eng.matmul(bY[:, 0:C], hT[:, k, :], w2[:, bass.ds(e * (KH * C) + k * C, C)],
                                            start=False, stop=(k == KH - 1))
                        done(i_, "down")
                steps(eng, body, NS, 4, 2)

            @block.scalar
            def _(eng):
                def body(on):
                    b = on(0)
                    if b:
                        need(eng, "up", b.at(1))
                        need(eng, "htr", b.at(-1))
                        done(eng.activation(hs[b.par][:, :], bH[b.par][:, :], ACT.Gelu), "gel")
                steps(eng, body, NS, 4, 2)

            @block.vector
            def _(eng):
                def body(on):
                    a, b = on(0), on(1)
                    if a:
                        need(eng, "gtr", a.at(1))
                        need(eng, "up", a.at(0))
                        done(eng.tensor_copy(gT[:, :, :], bT[:, 0:C].rearrange("p (a c) -> p a c", a=KC)), "gT")
                    if b:
                        need(eng, "htr", b.at(1))
                        need(eng, "down", b.at(0))
                        done(eng.tensor_copy(hT[:, :, :], bHT[b.par][:, :].rearrange("p (a c) -> p a c", a=KH)), "hT")
                        need(eng, "down", b.at(1))
                        need(eng, f"sca{b.par}", b.turn(0) * 16)
                        done(eng.scalar_tensor_tensor(yo[b.par][:, :], bY[:, 0:C], gr[b.par][:, 2 * C:2 * C + 1],
                                                      gr[b.par][:, C:2 * C], ALU.mult, ALU.add), "yo")
                steps(eng, body, NS, 4, 2)


_INS = ["x", "ctx_1024", "L0_xattn_Wq", "L0_xattn_bq", "L0_xattn_Wk", "L0_xattn_bk", "L0_xattn_Wv",
        "L0_xattn_bv", "L0_xattn_Wd", "L0_xattn_bd", "L0_ffn_w_red", "L0_ffn_wg", "L0_ffn_W1",
        "L0_ffn_b1", "L0_ffn_W2", "L0_ffn_b2"]


def kernel(**inputs):
    import numpy as np
    import concourse.bacc as bacc
    from concourse.bass_utils import run_bass_kernel_spmd

    nc = bacc.Bacc("TRN2", target_bir_lowering=False, num_devices=1)
    arrays, args = {}, []
    for name in _INS:
        a = np.ascontiguousarray(inputs[name])
        arrays[f"in_{name}"] = a
        args.append(nc.dram_tensor(f"in_{name}", a.shape, mybir.dt.from_np(a.dtype), kind="ExternalInput").ap())
    out = nc.dram_tensor("out", [NTOK, C], mybir.dt.float32, kind="ExternalOutput").ap()
    build(nc, *args, out)
    r = run_bass_kernel_spmd(nc, [arrays], core_ids=[0])
    return r.results[0]["out"].reshape(NT, P, C)
```

```python
import concourse.bass as bass
from concourse import mybir
from contextlib import ExitStack

P = 128
C = 256
NH = 16
HD = C // NH
NT = 32
NTOK = NT * P
NE = 8
HID = 512
NG = 16
KC = C // P
KH = HID // P
NS = NT + NE - 1
NSP = NS + 1
ROW = 2 * C + 4
BW = 4 * C
EPS = 1e-5
HALF = NH // 2
PVC = 4
PVJ = NH // PVC


class Tile:

    def __init__(self, unroll, i, c):
        self.unroll, self.i, self.c, self.par = unroll, i, c, c % 2

    def at(self, k=0):
        return self.c + k if self.i is None else self.i * self.unroll + (self.c + k)

    def slot(self, ring):
        return self.c % ring

    def turn(self, k=0, ring=2):
        n = self.c // ring + k
        return n if self.i is None else self.i * (self.unroll // ring) + n


def build(nc, x, ctx_in, Wq, bq, Wk, bk, Wv, bv, Wd, bd, w_red, wg, W1, b1, W2, b2, out):
    f32, bf16, i32 = mybir.dt.float32, mybir.dt.bfloat16, mybir.dt.int32
    ALU, ACT, AX = mybir.AluOpType, mybir.ActivationFunctionType, mybir.AxisListType.X

    attn_scr = nc.dram_tensor("attn_scr", [NT, NH, P, HD], f32, kind="Internal").ap()
    row_scr = nc.dram_tensor("row_scr", [NTOK, ROW], f32, kind="Internal").ap()
    bias_scr = nc.dram_tensor("bias_scr", [3, BW + NE * (HID + C)], bf16, kind="Internal").ap()
    NB = BW + NE * (HID + C)
    B1O, B2O = BW, BW + NE * HID

    es = ExitStack()
    with es:
        def sb(name, shape, dt=f32):
            return es.enter_context(nc.sbuf_tensor(name, shape, dt))

        sems = {}

        def sem(name):
            if name not in sems:
                sems[name] = es.enter_context(nc.semaphore(name))
            return sems[name]

        w1 = sb("w1", [P, NE * KC * HID])
        w2 = sb("w2", [P, NE * KH * C])
        wT = sb("wT", [P, KC, 4 * C])
        brow = sb("brow", [P, NB], bf16)
        ones = sb("ones", [P, P], bf16)
        ident = sb("ident", [P, P])
        gate = sb("gate", [P, KC, NE])
        half = sb("half", [P, 1])
        xt = [sb(f"xt{k}", [P, C]) for k in range(2)]
        ct = [sb(f"ct{k}", [P, C]) for k in range(2)]
        xr = [sb(f"xr{k}", [P, C]) for k in range(2)]
        ar = [sb(f"ar{k}", [P, C]) for k in range(2)]
        xn = sb("xn", [P, C])
        xcT = sb("xcT", [P, 4, P])
        q = [sb(f"q{k}", [P, C]) for k in range(2)]
        kk = [sb(f"kk{k}", [P, C]) for k in range(2)]
        prod = [sb(f"prod{k}", [P, HALF, C]) for k in range(2)]
        pv = [sb(f"pv{k}", [P, PVJ, C]) for k in range(PVC)]
        lg = sb("lg", [P, NH, NH])
        pr = sb("pr", [P, NH, NH])
        mx = sb("mx", [P, NH])
        sm = sb("sm", [P, NH])
        rsm = sb("rsm", [P, NH])
        ao = [sb(f"ao{k}", [P, NH, HD]) for k in range(2)]
        aoT = sb("aoT", [P, KC, P])
        x2T = sb("x2T", [P, KC, P])
        cat = [sb(f"cat{k}", [P, ROW]) for k in range(2)]
        st = [sb(f"st{k}", [P, 6]) for k in range(2)]
        mv = [sb(f"mv{k}", [P, 2]) for k in range(2)]
        ve = [sb(f"ve{k}", [P, 1]) for k in range(2)]
        rs = [sb(f"rs{k}", [P, 1]) for k in range(2)]
        gm = sb("gm", [P, 1])
        ge = sb("ge", [P, NE])
        gs = sb("gs", [P, 1])
        glog = sb("glog", [P, NT, NE])

        def bank(name):
            return es.enter_context(nc.psum_tensor(name, [P, 512], f32))

        bT, bQ, bO, bA, bY, bG = (bank(n) for n in ("bT", "bQ", "bO", "bA", "bY", "bG"))
        bKV = [bank("bKV0"), bank("bKV1")]

        def done(inst, ev, by=1):
            return inst.then_inc(sem(ev), by)

        def need(eng, ev, n):
            if not isinstance(n, int) or n > 0:
                eng.wait_ge(sem(ev), n)

        stage = pv[0][:, :, :].rearrange("p a b -> p (a b)")
        stage2 = pv[1][:, :, :].rearrange("p a b -> p (a b)")
        wst = [(stage if w < 2 else stage2)[:, (w % 2) * 512:(w % 2) * 512 + 512]
               .rearrange("p (a c) -> p a c", a=KC) for w in range(4)]
        NBC = NB // P
        bst = pv[2][:, 0, 0:NBC]
        bres = pv[2][:, 1, 0:NBC]
        bres2 = pv[2][:, 2, 0:NBC]
        bsp = pv[3][:, 0, :].bitcast(bf16)[:, 0:3 * NBC].rearrange("p (k f) -> p k f", k=3)
        wrp = pv[3][:, 1:3, 0:P]
        wgb = pv[3][:, 3, 0:NE * NG]
        wgs = pv[3][:, 3, NE * NG:2 * NE * NG]
        wgT = q[0][:, 0:NE]
        wrT = q[0][:, NE:NE]
        wrT = kk[0][:, :].rearrange("p (a c) -> p a c", a=KC)
        nrm = q[1][:, 0:NE]
        nr2 = q[1][:, NE:2 * NE]
        nr3 = q[1][:, 2 * NE:3 * NE]

        pieces = [(b, k * 2, 2, k * C) for k, b in enumerate((bq, bk, bv, bd))]
        pieces += [(b1.rearrange("e h -> (e h)"), 8, NE * HID // P, B1O),
                   (b2.rearrange("e h -> (e h)"), 8 + NE * HID // P, NE * C // P, B2O)]

        with nc.Block() as block:
            @block.sync
            def _(eng):
                for w, src in enumerate((Wq, Wk, Wv, Wd)):
                    done(eng.dma_start(wst[w], src.rearrange("(a p) c -> p a c", p=P)), "ld_w", 16)
                for src, o, n, _ in pieces:
                    done(eng.dma_start(bst[:, o:o + n], src.rearrange("(p f) -> p f", p=P)), "ld_b", 16)
                need(eng, "pad0", 1)
                done(eng.dma_start(wrp[:, :, 0:NG], w_red.rearrange("(a p) g -> p a g", p=P)), "ld_g", 16)
                done(eng.dma_start(wgb, wg.rearrange("e g -> (e g)").rearrange("(o n) -> o n", o=1)
                                   .broadcast_to((P, NE * NG))), "ld_g", 16)
                with nc.allow_non_contiguous_dma("wg transposed, 128 elements"):
                    done(eng.dma_start(wgT[0:NG, :], wg.rearrange("e g -> g e")), "ld_g", 16)
                need(eng, "bsplit", 1)
                for _, o, n, off in pieces:
                    done(eng.dma_start(bias_scr[:, off:off + n * P].rearrange("k (p f) -> p k f", p=P),
                                       bsp[:, :, o:o + n]), "st_b", 16)
                need(eng, "st_b", 16 * len(pieces))
                need(eng, "brow0", 1)
                done(eng.dma_start(brow[0:3, :], bias_scr), "ld_br", 16)
                need(eng, "ld_br", 16)

            @block.gpsimd
            def _(eng):
                done(eng.memset(ident[:, :], 0.0), "c_id")
                need(eng, "c_id", 1)
                done(eng.affine_select(out=ident[:, :], in_=ident[:, :], compare_op=ALU.not_equal, fill=1.0,
                                       base=0, pattern=[[-1, P]], channel_multiplier=1), "ident")
                done(eng.memset(wrp, 0.0), "pad0")
                eng.memset(ones[:, :], 1.0)
                eng.memset(half[:, :], -0.5)
                done(eng.memset(brow[:, :], 0.0), "brow0")

            @block.vector
            def _(eng):
                need(eng, "ld_b", 16 * len(pieces))
                done(eng.tensor_copy(bsp[:, 0, :], bst), "v0")
                need(eng, "v0", 1)
                done(eng.tensor_tensor(bres, bst, bsp[:, 0, :], ALU.subtract), "v0")
                need(eng, "v0", 2)
                done(eng.tensor_copy(bsp[:, 1, :], bres), "v0")
                need(eng, "v0", 3)
                done(eng.tensor_tensor(bres2, bres, bsp[:, 1, :], ALU.subtract), "v0")
                need(eng, "v0", 4)
                done(eng.tensor_copy(bsp[:, 2, :], bres2), "bsplit")
                need(eng, "ld_g", 48)
                done(eng.tensor_tensor(wgs, wgb, wgb, ALU.mult), "v0")
                need(eng, "v0", 5)
                done(eng.tensor_reduce(nrm, wgs.rearrange("p (e g) -> p e g", e=NE), AX, ALU.add), "nrm")
                need(eng, "nsq", 1)
                done(eng.tensor_scalar(nr3, nr2, 1e-4, None, ALU.max), "v0")
                need(eng, "v0", 6)
                done(eng.reciprocal(nrm, nr3), "v0")
                for w in range(4):
                    b = (bT, bQ, bO, bA)[w]
                    need(eng, "wtr", w + 1)
                    done(eng.tensor_copy(wT[:, :, w * C:(w + 1) * C],
                                         b[:, :].rearrange("p (a c) -> p a c", a=KC)), "v0")
                need(eng, "wrt", 1)
                done(eng.tensor_copy(wrT[:, :, :], bY[:, 0:C].rearrange("p (a c) -> p a c", a=KC)), "wrTs")
                need(eng, "gmm", 1)
                need(eng, "v0", 7)
                done(eng.tensor_tensor(gate[:, :, :], bG[:, 0:KC * NE].rearrange("p (a e) -> p a e", a=KC),
                                       nrm.unsqueeze(1).broadcast_to((P, KC, NE)), ALU.mult), "v0")

            @block.scalar
            def _(eng):
                for s_, d_ in ((W1, w1), (W2, w2)):
                    k_ = KC if d_ is w1 else KH
                    dv = d_[:, :].rearrange("p (e k n) -> p e k n", e=NE, k=k_)
                    for e in range(NE):
                        done(eng.dma_start(dv[:, e, :, :], s_[e].rearrange("(k p) n -> p k n", p=P)),
                             "ld_moe", 16)
                need(eng, "nrm", 1)
                done(eng.activation(nr2, nrm, ACT.Sqrt), "nsq")

            @block.tensor
            def _(eng):
                need(eng, "ident", 1)
                need(eng, "ld_w", 64)
                for w in range(4):
                    b = (bT, bQ, bO, bA)[w]
                    for a in range(KC):
                        for c in range(KC):
                            i_ = eng.transpose(b[:, c * C + a * P:c * C + (a + 1) * P],
                                               wst[w][:, a, c * P:(c + 1) * P], ident[:, :])
                    done(i_, "wtr")
                need(eng, "ld_g", 48)
                for a in range(KC):
                    i_ = eng.transpose(bY[:, a * P:(a + 1) * P], wrp[:, a, :], ident[:, :])
                done(i_, "wrt")
                need(eng, "wrTs", 1)
                for a in range(KC):
                    i_ = eng.matmul(bG[:, a * NE:(a + 1) * NE], wrT[0:NG, a, :], wgT[0:NG, :],
                                    start=True, stop=True)
                done(i_, "gmm")

        LAGS, FIRST = 6, 8

        def steps(eng, body, total, first, lags, unroll=2, lead=0):
            def step(i, c):
                def on(lag):
                    n = Tile(unroll, i, c - lag)
                    return n if i is not None or 0 <= c - lag < total else None
                body(on)
            last = first + (total - lead - first) // unroll * unroll
            for c in range(first):
                step(None, c)
            with eng.Fori(0, (last - first) // unroll) as i:
                for u in range(unroll):
                    step(i, first + u)
            for c in range(last, total + lags):
                step(None, c)

        with nc.Block() as block:
            @block.sync
            def _(eng):
                def body(on):
                    nxt, a, e, c, g = on(-1), on(0), on(3), on(4), on(6)
                    if g:
                        need(eng, "score", g.at(1))
                        done(eng.dma_start(row_scr[bass.ds(g.at() * P, P), :], cat[g.par][:, :]),
                             f"st_r{g.par}", 16)
                    for n in (nxt,):
                        if n:
                            need(eng, "xn", n.at(-1))
                            done(eng.dma_start(xt[n.par][:, :], x[n.at()]), f"ld_x{n.par}", 16)
                            need(eng, "tr_c", n.at(-1))
                            done(eng.dma_start(ct[n.par][:, :], ctx_in[n.at()]), f"ld_c{n.par}", 16)
                    if c:
                        need(eng, "x2", c.at(-1))
                        done(eng.dma_start(xr[c.par][:, :], x[c.at()]), f"ld_xr{c.par}", 16)
                    if e:
                        need(eng, "onorm", e.at(1))
                        done(eng.dma_start(attn_scr[e.at()].rearrange("i t d -> t i d"), ao[e.par][:, :, :]),
                             f"st_a{e.par}", 16)
                        need(eng, f"st_a{e.par}", e.turn(1) * 16)
                        need(eng, "tr_a", e.at(-1))
                        done(eng.dma_start(ar[e.par][:, :], attn_scr[e.at()]
                                           .rearrange("i (a b) d -> (i a) (b d)", b=NH)), f"ld_a{e.par}", 16)
                body(lambda lag: Tile(2, None, 0) if lag == -1 else None)
                steps(eng, body, NT, FIRST, LAGS, lead=1)
                for k in range(2):
                    need(eng, f"st_r{k}", NT // 2 * 16)

            @block.gpsimd
            def _(eng):
                def power(n, w):
                    if n:
                        need(eng, f"ve{w}", n.at(1))
                        need(eng, "xn" if w == 0 else "x2n", n.at(0))
                        done(eng.tensor_tensor(rs[w][:, :], ve[w][:, :], half[:, :], ALU.pow), f"rs{w}")

                def products(n, h):
                    if n:
                        if h == 0:
                            need(eng, "kcp", n.at(1))
                        need(eng, f"qkred{h}", n.at(0))
                        done(eng.tensor_tensor(
                            prod[h][:, :, :].rearrange("p i (j d) -> p i j d", j=NH),
                            q[n.par][:, h * HALF * HD:(h + 1) * HALF * HD].rearrange("p (i d) -> p i d", d=HD)
                            .unsqueeze(2).broadcast_to((P, HALF, NH, HD)),
                            kk[n.par][:, :].rearrange("p (j d) -> p j d", d=HD)
                            .unsqueeze(1).broadcast_to((P, HALF, NH, HD)), ALU.mult), f"qk{h}")

                def body(on):
                    power(on(0), 0)
                    products(on(1), 0)
                    power(on(4), 1)
                    products(on(1), 1)
                steps(eng, body, NT, FIRST, LAGS)

            @block.vector
            def _(eng):
                def body(on):
                    a, b, e, c, d = (on(k) for k in (0, 2, 3, 4, 5))

                    def qk_sum(h):
                        need(eng, f"qk{h}", b.at(1))
                        done(eng.tensor_reduce(lg[:, h * HALF:(h + 1) * HALF, :],
                                               prod[h][:, :, :].rearrange("p i (j d) -> p i j d", j=NH),
                                               AX, ALU.add), f"qkred{h}")

                    def pv_mult(g):
                        need(eng, f"pvm{g}", b.at(0))
                        v = bKV[b.par][:, C + g * PVJ * HD:C + (g + 1) * PVJ * HD]
                        done(eng.tensor_tensor(
                            pv[g][:, :, :].rearrange("p j (i d) -> p j i d", i=NH),
                            v.rearrange("p (j d) -> p j d", d=HD).unsqueeze(2).broadcast_to((P, PVJ, NH, HD)),
                            pr[:, :, g * PVJ:(g + 1) * PVJ].rearrange("p i j -> p j i")
                            .unsqueeze(3).broadcast_to((P, PVJ, NH, HD)), ALU.mult), f"pv{g}")

                    if a:
                        need(eng, f"ld_x{a.par}", a.turn(1) * 16)
                        done(eng.bn_stats(st[0][:, :], xt[a.par][:, :]), "st0")
                        need(eng, "st0", a.at(1))
                    if b:
                        qk_sum(0)
                    if a:
                        done(eng.bn_aggr(mv[0][:, :], st[0][:, :]), "mv0")
                        need(eng, "mv0", a.at(1))
                        need(eng, "rs0", a.at(0))
                        done(eng.tensor_scalar(ve[0][:, :], mv[0][:, 1:2], EPS, None, ALU.add), "ve0")
                    if b:
                        qk_sum(1)
                        need(eng, "qkred1", b.at(1))
                        done(eng.tensor_reduce(mx[:, :], lg[:, :, :], AX, ALU.max), "mx")
                    if a:
                        need(eng, "rs0", a.at(1))
                        need(eng, "tr_in", a.at(0))
                        done(eng.tensor_scalar(xn[:, :], xt[a.par][:, :], mv[0][:, 0:1], rs[0][:, :],
                                               ALU.subtract, ALU.mult), "xn")
                    if b:
                        need(eng, "mx", b.at(1))
                        done(eng.tensor_tensor(lg[:, :, :], lg[:, :, :],
                                               mx[:, :].unsqueeze(2).broadcast_to((P, NH, NH)),
                                               ALU.subtract), "lsub")
                    if e:
                        need(eng, f"pvm{PVC - 1}", e.at(1))
                        need(eng, f"st_a{e.par}", e.turn(0) * 16)
                        need(eng, "rsm", e.at(1))
                        done(eng.tensor_tensor(ao[e.par][:, :, :], bO[:, 0:C].rearrange("p (i d) -> p i d", i=NH),
                                               rsm[:, :].unsqueeze(2).broadcast_to((P, NH, HD)), ALU.mult), "onorm")
                    if c:
                        need(eng, f"ld_xr{c.par}", c.turn(1) * 16)
                        need(eng, "wd", c.at(1))
                        need(eng, f"st_r{c.par}", c.turn(0) * 16)
                        done(eng.tensor_tensor(cat[c.par][:, C:2 * C], bY[:, 0:C], xr[c.par][:, :], ALU.add), "x2")
                        need(eng, "x2", c.at(1))
                        done(eng.bn_stats(st[1][:, :], cat[c.par][:, C:2 * C]), "st1")
                        need(eng, "st1", c.at(1))
                    if b:
                        need(eng, "exp", b.at(1))
                        done(eng.tensor_reduce(sm[:, :], pr[:, :, :], AX, ALU.add), "sm")
                    if c:
                        done(eng.bn_aggr(mv[1][:, :], st[1][:, :]), "mv1")
                        need(eng, "mv1", c.at(1))
                        need(eng, "rs1", c.at(0))
                        done(eng.tensor_scalar(ve[1][:, :], mv[1][:, 1:2], EPS, None, ALU.add), "ve1")
                    if b:
                        pv_mult(0)
                        need(eng, "sm", b.at(1))
                        need(eng, "onorm", b.at(0))
                        done(eng.reciprocal(rsm[:, :], sm[:, :]), "rsm")
                        pv_mult(1)
                        pv_mult(2)
                    if c:
                        need(eng, "rs1", c.at(1))
                        done(eng.tensor_scalar(cat[c.par][:, 0:C], cat[c.par][:, C:2 * C], mv[1][:, 0:1],
                                               rs[1][:, :], ALU.subtract, ALU.mult), "x2n")
                    if d:
                        need(eng, "glg", d.at(1))
                        done(eng.tensor_reduce(gm[:, :], bG[:, C:C + NE], AX, ALU.max), "gm")
                        need(eng, "gm", d.at(1))
                        done(eng.tensor_scalar(glog[:, d.at(), :], bG[:, C:C + NE], gm[:, :], None,
                                               ALU.subtract), "gsub")
                    if b:
                        pv_mult(3)
                    if d:
                        need(eng, "gexp", d.at(1))
                        done(eng.reciprocal(cat[d.par][:, 2 * C:2 * C + 1], gs[:, :]), "score")
                for k in range(2):
                    eng.memset(cat[k][:, 2 * C:ROW], 0.0)
                steps(eng, body, NT, FIRST, LAGS)

            @block.scalar
            def _(eng):
                def body(on):
                    p, a, b, c, d = (on(k) for k in (1, 0, 2, 4, 5))
                    if c:
                        need(eng, "tr_a", c.at(1))
                        need(eng, "wd", c.at(0))
                        done(eng.activation(aoT[:, :, :], bA[:, 0:C].rearrange("p (a c) -> p a c", a=KC),
                                            ACT.Copy), "aoT")
                    if d:
                        need(eng, "tr_g", d.at(1))
                        need(eng, "glg", d.at(0))
                        done(eng.activation(x2T[:, :, :], bG[:, 0:C].rearrange("p (a c) -> p a c", a=KC),
                                            ACT.Copy), "x2T")
                    if b:
                        need(eng, "lsub", b.at(1))
                        need(eng, f"pv{PVC - 1}", b.at(0))
                        done(eng.activation(pr[:, :, :], lg[:, :, :], ACT.Exp, scale=HD ** -0.5), "exp")
                    if a:
                        need(eng, "tr_in", a.at(1))
                        need(eng, "kv", a.at(0))
                        done(eng.activation(xcT[:, :, :], bT[:, :].rearrange("p (a c) -> p a c", a=4),
                                            ACT.Copy), "xcT")
                    if d:
                        need(eng, "gsub", d.at(1))
                        done(eng.activation(ge[:, :], glog[:, d.at(), :], ACT.Exp, accum_out=gs[:, :]), "gexp")
                    if a:
                        need(eng, "qq", a.at(1))
                        need(eng, "qk1", a.at(-1))
                        done(eng.activation(q[a.par][:, :], bQ[:, 0:C], ACT.Copy), "qcp")
                        need(eng, "kv", a.at(1))
                        done(eng.activation(kk[a.par][:, :], bKV[a.par][:, 0:C], ACT.Copy), "kcp")
                steps(eng, body, NT, FIRST, LAGS)
                need(eng, "ld_moe", 16 * 2 * NE)

            @block.tensor
            def _(eng):
                def bias(dst, off, n):
                    return eng.matmul(dst, ones[:, :], brow[:, off:off + n], start=True, stop=False)

                def body(on):
                    a, b, c, d = (on(k) for k in (0, 2, 4, 5))

                    def pv_sum(g):
                        need(eng, f"pv{g}", b.at(1))
                        for j in range(PVJ):
                            i_ = eng.matmul(bO[:, 0:C], ident[:, :], pv[g][:, j, :],
                                            start=(g == 0 and j == 0), stop=(g == PVC - 1 and j == PVJ - 1))
                        done(i_, f"pvm{g}")

                    if a:
                        need(eng, f"ld_c{a.par}", a.turn(1) * 16)
                        need(eng, "xcT", a.at(0))
                        for k in range(KC):
                            i_ = eng.transpose(bT[:, (KC + k) * P:(KC + k + 1) * P],
                                               ct[a.par][:, k * P:(k + 1) * P], ident[:, :])
                        done(i_, "tr_c")
                    if d:
                        need(eng, "x2n", d.at(1))
                        need(eng, "gsub", d.at(0))
                        for k in range(KC):
                            i_ = eng.transpose(bG[:, k * P:(k + 1) * P], cat[d.par][:, k * P:(k + 1) * P],
                                               ident[:, :])
                        done(i_, "tr_g")
                    if c:
                        need(eng, f"ld_a{c.par}", c.turn(1) * 16)
                        need(eng, "aoT", c.at(0))
                        for k in range(KC):
                            i_ = eng.transpose(bA[:, k * P:(k + 1) * P], ar[c.par][:, k * P:(k + 1) * P],
                                               ident[:, :])
                        done(i_, "tr_a")
                    if d:
                        need(eng, "x2T", d.at(1))
                        for k in range(KC):
                            i_ = eng.matmul(bG[:, C:C + NE], x2T[:, k, :], gate[:, k, :],
                                            start=(k == 0), stop=(k == KC - 1))
                        done(i_, "glg")
                    if c:
                        need(eng, "aoT", c.at(1))
                        need(eng, "x2", c.at(0))
                        bias(bY[:, 0:C], 3 * C, C)
                        for k in range(KC):
                            i_ = eng.matmul(bY[:, 0:C], aoT[:, k, :], wT[:, k, 3 * C:4 * C],
                                            start=False, stop=(k == KC - 1))
                        done(i_, "wd")
                    if a:
                        need(eng, "xn", a.at(1))
                        for k in range(KC):
                            i_ = eng.transpose(bT[:, k * P:(k + 1) * P], xn[:, k * P:(k + 1) * P], ident[:, :])
                        done(i_, "tr_in")
                        need(eng, "qcp", a.at(0))
                        bias(bQ[:, 0:C], 0, C)
                        need(eng, "xcT", a.at(1))
                        for k in range(KC):
                            i_ = eng.matmul(bQ[:, 0:C], xcT[:, k, :], wT[:, k, 0:C], start=False, stop=(k == KC - 1))
                        done(i_, "qq")
                    if b:
                        need(eng, "onorm", b.at(0))
                        pv_sum(0)
                        pv_sum(1)
                        pv_sum(2)
                    if a:
                        need(eng, f"pv{PVC - 1}", a.at(-1))
                        need(eng, "kcp", a.at(-1))
                        bias(bKV[a.par][:, :], C, 2 * C)
                        for k in range(KC):
                            i_ = eng.matmul(bKV[a.par][:, :], xcT[:, KC + k, :], wT[:, k, C:3 * C],
                                            start=False, stop=(k == KC - 1))
                        done(i_, "kv")
                    if b:
                        pv_sum(3)
                steps(eng, body, NT, FIRST, LAGS)

        def fl(t):
            return t[:, :, :].rearrange("p a b -> p (a b)")

        r0, r1 = fl(prod[0]), fl(prod[1])
        oh = sb("oh", [P, NT, NE], bf16)
        tri = sb("tri", [P, P], bf16)
        idg = sb("idg", [P, NSP], i32)
        ids = sb("ids", [P, NSP], i32)
        texp = sb("texp", [P, NSP], i32)
        io_e = r0[:, 0:256].rearrange("p (n e) -> p n e", e=NE)
        io_m = r0[:, 256:512].rearrange("p (e m) -> p e m", e=NE)
        io_r = r0[:, 512:640]
        io_k = r0[:, 640:640 + NSP]
        seg = r0[:, 704:960].rearrange("p (e n) -> p e n", e=NE)
        one8 = r0[:, 960:960 + NE]
        pid = r0[:, 970:971]
        io_n = r0[:, 992:992 + NT]
        key = r0[:, 1024:1280].rearrange("p (n e) -> p n e", e=NE)
        top = r0[:, 1280:1280 + NT]
        tot = r0[:, 1312:1568].rearrange("p (e n) -> p e n", e=NE)
        inc = r0[:, 1568:1824].rearrange("p (e n) -> p e n", e=NE)
        til = r0[:, 1824:1824 + NE]
        tinc = r0[:, 1840:1840 + NE]
        texc = r0[:, 1856:1856 + NE]
        gtm = r1[:, 0:256].rearrange("p (e m) -> p e m", e=NE)
        exc = r1[:, 256:512].rearrange("p (e n) -> p e n", e=NE)
        slot = r1[:, 512:768].rearrange("p (n e) -> p n e", e=NE)
        pos = r1[:, 768:800]
        posr = r1[:, 800:832]
        posk = r1[:, 832:864]
        pint = r1[:, 864:896].bitcast(i32)
        pir = r1[:, 896:928].bitcast(i32)
        pik = r1[:, 928:960].bitcast(i32)
        tcmp = r1[:, 960:960 + NSP * NE].rearrange("p (k e) -> p k e", e=NE)
        tsum = r1[:, 1280:1280 + NSP]
        tmin = r1[:, 1320:1320 + NSP]
        inv = r1[:, 1360:1360 + NSP]
        emp = r1[:, 1400:1400 + NSP]
        inv2 = r1[:, 1440:1440 + NSP]
        selr = [pv[k][:, :, :].rearrange("p a b -> p (a b)").bitcast(bf16)
                .rearrange("p (n r) -> p n r", r=P) for k in range(2)]
        selk = [pv[2 + k][:, :, :].rearrange("p a b -> p (a b)").bitcast(bf16)[:, 0:16 * 3 * NSP]
                .rearrange("p (n w k) -> p n w k", w=3, k=NSP) for k in range(2)]

        with nc.Block() as block:
            @block.gpsimd
            def _(eng):
                eng.iota(io_e, [[0, NT], [-1, NE]], base=NE, channel_multiplier=0, allow_small_or_imprecise_dtypes=True)
                eng.iota(io_m, [[0, NE], [P, NT]], base=0, channel_multiplier=0, allow_small_or_imprecise_dtypes=True)
                eng.iota(io_r, [[1, P]], base=0, channel_multiplier=0, allow_small_or_imprecise_dtypes=True)
                eng.iota(io_k, [[1, NSP]], base=0, channel_multiplier=0, allow_small_or_imprecise_dtypes=True)
                eng.iota(io_n, [[1, NT]], base=0, channel_multiplier=0, allow_small_or_imprecise_dtypes=True)
                eng.iota(pid, [[0, 1]], base=0, channel_multiplier=1, allow_small_or_imprecise_dtypes=True)
                eng.memset(one8, 1.0)
                eng.memset(seg, 1.0)
                done(eng.memset(tri[:, :], 1.0), "rc0")
                need(eng, "rc0", 1)
                done(eng.memset(seg[:, :, 0:1], 0.0), "rc1")
                done(eng.affine_select(out=tri[:, :], in_=tri[:, :], compare_op=ALU.is_gt, fill=0.0, base=0,
                                       pattern=[[1, P]], channel_multiplier=-1), "rconst")

            @block.vector
            def _(eng):
                steps_ = [0]

                def then(i_):
                    steps_[0] += 1
                    done(i_, "rv")
                    need(eng, "rv", steps_[0])

                need(eng, "rconst", 1)
                then(eng.scalar_tensor_tensor(key, glog[:, :, :], 0.0, io_e, ALU.is_ge, ALU.mult))
                then(eng.tensor_reduce(top, key, AX, ALU.max))
                done(eng.tensor_tensor(oh[:, :, :], key, top.unsqueeze(2).broadcast_to((P, NT, NE)),
                                       ALU.is_equal), "oh")
                need(eng, "cnt", 1)
                then(eng.tensor_copy(tot, bT[:, 0:NT * NE].rearrange("p (n e) -> p e n", e=NE)))
                then(eng.tensor_tensor_scan(inc.rearrange("p e n -> p (e n)"), seg.rearrange("p e n -> p (e n)"),
                                            tot.rearrange("p e n -> p (e n)"), 0.0, ALU.mult, ALU.add))
                then(eng.tensor_tensor(gtm, inc[:, :, NT - 1:NT].broadcast_to((P, NE, NT)), io_m, ALU.is_gt))
                then(eng.tensor_reduce(til, gtm, AX, ALU.add))
                then(eng.tensor_tensor_scan(tinc, one8, til, 0.0, ALU.mult, ALU.add))
                then(eng.tensor_tensor(tcmp, tinc.unsqueeze(1).broadcast_to((P, NSP, NE)),
                                       io_k.unsqueeze(2).broadcast_to((P, NSP, NE)), ALU.is_le))
                then(eng.tensor_reduce(tsum, tcmp, AX, ALU.add))
                then(eng.tensor_scalar(tmin, tsum, float(NE - 1), None, ALU.min))
                done(eng.tensor_copy(texp[:, :], tmin), "texp")
                then(eng.tensor_tensor(texc, tinc, til, ALU.subtract))
                then(eng.tensor_tensor(exc, inc, tot, ALU.subtract))
                then(eng.scalar_tensor_tensor(inc, texc.unsqueeze(2).broadcast_to((P, NE, NT)), float(P), exc,
                                              ALU.mult, ALU.add))
                then(eng.tensor_tensor(slot, bQ[:, 0:NT * NE].rearrange("p (n e) -> p n e", e=NE),
                                       inc.rearrange("p e n -> p n e"), ALU.add))
                then(eng.tensor_tensor(slot, slot, oh[:, :, :], ALU.mult))
                then(eng.tensor_reduce(pos, slot, AX, ALU.add))
                then(eng.tensor_copy(pint, pos))
                then(eng.tensor_scalar(pir, pint, P - 1, None, ALU.bitwise_and))
                then(eng.tensor_scalar(pik, pint, P.bit_length() - 1, None, ALU.logical_shift_right))
                then(eng.tensor_copy(posr, pir))
                then(eng.tensor_copy(posk, pik))
                for k in range(2):
                    n = slice(k * 16, k * 16 + 16)
                    done(eng.tensor_tensor(selr[k], io_r.unsqueeze(1).broadcast_to((P, 16, P)),
                                           posr[:, n].unsqueeze(2).broadcast_to((P, 16, P)), ALU.is_equal), "selr")
                    then(eng.tensor_tensor(selk[k][:, :, 0, :], io_k.unsqueeze(1).broadcast_to((P, 16, NSP)),
                                           posk[:, n].unsqueeze(2).broadcast_to((P, 16, NSP)), ALU.is_equal))
                    done(eng.tensor_scalar(selk[k][:, :, 1, :], selk[k][:, :, 0, :], pid, None, ALU.mult), "selp")
                    done(eng.tensor_tensor(selk[k][:, :, 2, :], selk[k][:, :, 0, :],
                                           io_n[:, n].unsqueeze(2).broadcast_to((P, 16, NSP)), ALU.mult), "selk")
                need(eng, "invmm", 1)
                then(eng.tensor_copy(inv2, bO[:, NSP:2 * NSP]))
                then(eng.scalar_tensor_tensor(inv, bO[:, 2 * NSP:3 * NSP], float(P), inv2, ALU.mult, ALU.add))
                then(eng.tensor_scalar(emp, bO[:, 0:NSP], -float(NTOK), float(NTOK), ALU.mult, ALU.add))
                then(eng.tensor_tensor(emp, emp, inv, ALU.add))
                done(eng.tensor_copy(idg[:, :], inv), "inv")
                done(eng.tensor_copy(ids[:, :], emp), "inv")

            @block.tensor
            def _(eng):
                need(eng, "oh", 1)
                need(eng, "rconst", 1)
                ohf = oh[:, :, :].rearrange("p n e -> p (n e)")
                eng.matmul(bQ[:, 0:NT * NE], tri[:, :], ohf, start=True, stop=True)
                done(eng.matmul(bT[:, 0:NT * NE], ones[:, :], ohf, start=True, stop=True), "cnt")
                for n in range(NT):
                    k = n // 16
                    if n % 16 == 0:
                        need(eng, "selk", k + 1)
                    i_ = eng.matmul(bO[:, 0:3 * NSP], selr[k][:, n % 16, :],
                                    selk[k][:, n % 16, :, :].rearrange("p w k -> p (w k)"),
                                    start=(n == 0), stop=(n == NT - 1))
                done(i_, "invmm")

        RB, FIRSTB, LAGSB = 4, 8, 4
        ig = [sb(f"ig{k}", [P, 1], i32) for k in range(RB)]
        isc = [sb(f"isc{k}", [P, 1], i32) for k in range(RB)]
        gr = [sb(f"gr{k}", [P, ROW]) for k in range(RB)]
        yo = [sb(f"yo{k}", [P, C]) for k in range(RB)]
        gT = [sb(f"gT{k}", [P, KC, P]) for k in range(2)]
        hs = [sb(f"hs{k}", [P, HID]) for k in range(2)]
        hT = [sb(f"hT{k}", [P, KH, P]) for k in range(2)]
        held = sb("held", [P, 2])
        bH, bHT, bX, bYB = [bO, bA], bKV, [bT, bQ], [bY, bG]

        with nc.Block() as block:
            @block.gpsimd
            def _(eng):
                def hold(k):
                    eng.tensor_tensor(held[:, k:k + 1], half[:, :], half[:, :], ALU.add)

                need(eng, "inv", 2)

                def body(on):
                    a, c = on(0), on(4)
                    if a:
                        k, at = a.slot(RB), eng.snap(a.at())
                        need(eng, f"gat{k}", a.turn(0, RB) * 16)
                        done(eng.tensor_copy(ig[k][:, :], idg[:, bass.ds(at, 1)]), "ig")
                    if c:
                        k, at = c.slot(RB), eng.snap(c.at())
                        need(eng, f"sca{k}", c.turn(0, RB) * 16)
                        done(eng.tensor_copy(isc[k][:, :], ids[:, bass.ds(at, 1)]), "isc")
                    if a:
                        k = a.slot(RB)
                        need(eng, "ig", a.at(1))
                        need(eng, "yo", a.at(1 - RB))
                        hold(0)
                        done(eng.indirect_dma_start(gr[k][:, :], None, row_scr,
                                                    bass.IndirectOffsetOnAxis(ap=ig[k][:, :], axis=0)),
                             f"gat{k}", 16)
                    if c:
                        k = c.slot(RB)
                        need(eng, "isc", c.at(1))
                        need(eng, "yo", c.at(1))
                        hold(1)
                        done(eng.indirect_dma_start(out, bass.IndirectOffsetOnAxis(ap=isc[k][:, :], axis=0),
                                                    yo[k][:, :], None, bounds_check=NTOK - 1,
                                                    oob_is_err=False), f"sca{k}", 16)
                steps(eng, body, NS, FIRSTB, LAGSB, RB)
                for k in range(RB):
                    need(eng, f"sca{k}", len(range(k, NS, RB)) * 16)

            @block.tensor
            def _(eng):
                def body(on):
                    x_, a, b = on(1), on(2), on(3)
                    if b:
                        eb = eng.value_load(texp[0:1, bass.ds(b.at(), 1)], min_val=0, max_val=NE - 1)
                        need(eng, "gel", b.at(1))
                        need(eng, "hT", b.at(-1))
                        for k in range(KH):
                            i_ = eng.transpose(bHT[b.par][:, k * P:(k + 1) * P],
                                               hs[b.par][:, k * P:(k + 1) * P], ident[:, :])
                        done(i_, "htr")
                    if a:
                        ea = eng.value_load(texp[0:1, bass.ds(a.at(), 1)], min_val=0, max_val=NE - 1)
                        need(eng, "gel", a.at(-1))
                        eng.matmul(bH[a.par][:, :], ones[:, :], brow[:, bass.ds(ea * HID + B1O, HID)],
                                   start=True, stop=False)
                        need(eng, "gT", a.at(1))
                        for k in range(KC):
                            i_ = eng.matmul(bH[a.par][:, :], gT[a.par][:, k, :],
                                            w1[:, bass.ds(ea * (KC * HID) + k * HID, HID)],
                                            start=False, stop=(k == KC - 1))
                        done(i_, "up")
                    if x_:
                        need(eng, f"gat{x_.slot(RB)}", x_.turn(1, RB) * 16)
                        need(eng, "gT", x_.at(-1))
                        for k in range(KC):
                            i_ = eng.transpose(bX[x_.par][:, k * P:(k + 1) * P],
                                               gr[x_.slot(RB)][:, k * P:(k + 1) * P], ident[:, :])
                        done(i_, "gtr")
                    if b:
                        need(eng, "yo", b.at(-1))
                        eng.matmul(bYB[b.par][:, 0:C], ones[:, :], brow[:, bass.ds(eb * C + B2O, C)],
                                   start=True, stop=False)
                        need(eng, "hT", b.at(1))
                        for k in range(KH):
                            i_ = eng.matmul(bYB[b.par][:, 0:C], hT[b.par][:, k, :],
                                            w2[:, bass.ds(eb * (KH * C) + k * C, C)],
                                            start=False, stop=(k == KH - 1))
                        done(i_, "down")
                steps(eng, body, NS, FIRSTB, LAGSB, RB)

            @block.scalar
            def _(eng):
                def body(on):
                    a = on(2)
                    if a:
                        need(eng, "up", a.at(1))
                        need(eng, "htr", a.at(-1))
                        done(eng.activation(hs[a.par][:, :], bH[a.par][:, :], ACT.Gelu), "gel")
                steps(eng, body, NS, FIRSTB, LAGSB, RB)

            @block.vector
            def _(eng):
                def body(on):
                    x_, b = on(1), on(3)
                    if b:
                        need(eng, "htr", b.at(1))
                        need(eng, "down", b.at(-1))
                        done(eng.tensor_copy(hT[b.par][:, :, :],
                                             bHT[b.par][:, :].rearrange("p (a c) -> p a c", a=KH)), "hT")
                    if x_:
                        need(eng, "gtr", x_.at(1))
                        need(eng, "up", x_.at(-1))
                        done(eng.tensor_copy(gT[x_.par][:, :, :],
                                             bX[x_.par][:, 0:C].rearrange("p (a c) -> p a c", a=KC)), "gT")
                    if b:
                        k = b.slot(RB)
                        need(eng, "down", b.at(1))
                        need(eng, f"sca{k}", b.turn(0, RB) * 16)
                        done(eng.scalar_tensor_tensor(yo[k][:, :], bYB[b.par][:, 0:C], gr[k][:, 2 * C:2 * C + 1],
                                                      gr[k][:, C:2 * C], ALU.mult, ALU.add), "yo")
                steps(eng, body, NS, FIRSTB, LAGSB, RB)


_INS = ["x", "ctx_1024", "L0_xattn_Wq", "L0_xattn_bq", "L0_xattn_Wk", "L0_xattn_bk", "L0_xattn_Wv",
        "L0_xattn_bv", "L0_xattn_Wd", "L0_xattn_bd", "L0_ffn_w_red", "L0_ffn_wg", "L0_ffn_W1",
        "L0_ffn_b1", "L0_ffn_W2", "L0_ffn_b2"]


def kernel(**inputs):
    import numpy as np
    import concourse.bacc as bacc
    from concourse.bass_utils import run_bass_kernel_spmd

    nc = bacc.Bacc("TRN2", target_bir_lowering=False, num_devices=1)
    arrays, args = {}, []
    for name in _INS:
        a = np.ascontiguousarray(inputs[name])
        arrays[f"in_{name}"] = a
        args.append(nc.dram_tensor(f"in_{name}", a.shape, mybir.dt.from_np(a.dtype), kind="ExternalInput").ap())
    out = nc.dram_tensor("out", [NTOK, C], mybir.dt.float32, kind="ExternalOutput").ap()
    build(nc, *args, out)
    r = run_bass_kernel_spmd(nc, [arrays], core_ids=[0])
    return r.results[0]["out"].reshape(NT, P, C)
```

```python
import concourse.bass as bass
from concourse import mybir
from contextlib import ExitStack

P = 128
C = 256
NH = 16
HD = C // NH
NT = 32
NTOK = NT * P
NE = 8
HID = 512
NG = 16
KC = C // P
KH = HID // P
NS = NT + NE - 1
NSP = NS + 1
ROW = 2 * C + 4
BW = 4 * C
EPS = 1e-5
HALF = NH // 2
W1W = KC * HID + KH
PVH = [(0, 5), (5, 9), (9, 13), (13, 16)]
FOLD = (2, 0, 0, 0)
PVD, PVG = range(len(PVH) - 1), len(PVH) - 1


class Tile:

    def __init__(self, unroll, i, c):
        self.unroll, self.i, self.c, self.par = unroll, i, c, c % 2

    def at(self, k=0):
        return self.c + k if self.i is None else self.i * self.unroll + (self.c + k)

    def slot(self, ring):
        return self.c % ring

    def turn(self, k=0, ring=2):
        n = self.c // ring + k
        return n if self.i is None else self.i * (self.unroll // ring) + n


def build(nc, x, ctx_in, Wq, bq, Wk, bk, Wv, bv, Wd, bd, w_red, wg, W1, b1, W2, b2, out):
    f32, bf16, i32 = mybir.dt.float32, mybir.dt.bfloat16, mybir.dt.int32
    ALU, ACT, AX = mybir.AluOpType, mybir.ActivationFunctionType, mybir.AxisListType.X

    attn_scr = nc.dram_tensor("attn_scr", [NT, NH, P, HD], f32, kind="Internal").ap()
    row_scr = nc.dram_tensor("row_scr", [NTOK, ROW], f32, kind="Internal").ap()
    bias_scr = nc.dram_tensor("bias_scr", [3, BW], bf16, kind="Internal").ap()

    es = ExitStack()
    with es:
        def sb(name, shape, dt=f32):
            return es.enter_context(nc.sbuf_tensor(name, shape, dt))

        sems = {}

        def sem(name):
            if name not in sems:
                sems[name] = es.enter_context(nc.semaphore(name))
            return sems[name]

        w1b = sb("w1b", [P, NE, W1W])
        b2b = sb("b2b", [P, NE * C])
        w1f = w1b[:, :, :].rearrange("p e n -> p (e n)")
        w2 = sb("w2", [P, NE * KH * C])
        wT = sb("wT", [P, KC, 4 * C])
        brow = sb("brow", [P, BW], bf16)
        ones = sb("ones", [P, P], bf16)
        ident = sb("ident", [P, P])
        gate = sb("gate", [P, KC, NE])
        w1s = [sb(f"w1s{k}", [P, W1W]) for k in range(2)]
        half = sb("half", [P, 1])
        half8 = sb("half8", [P, NE])
        tri = sb("tri", [P, P], bf16)
        io_e = sb("io_e", [P, NT, NE])
        io_m = sb("io_m", [P, NE, NT])
        io_r = sb("io_r", [P, P, NT // 2], bf16)
        io_k = sb("io_k", [P, NSP, NT // 2], bf16)
        io_r1 = sb("io_r1", [P, P])
        io_k1 = sb("io_k1", [P, NSP])
        io_n = sb("io_n", [P, NT], bf16)
        pid = sb("pid", [P, 1])
        seg = sb("seg", [P, NE, NT])
        one8 = sb("one8", [P, NE])
        xt = [sb(f"xt{k}", [P, C]) for k in range(2)]
        ct = [sb(f"ct{k}", [P, C]) for k in range(2)]
        xr = [sb(f"xr{k}", [P, C]) for k in range(2)]
        ar = [sb(f"ar{k}", [P, C]) for k in range(2)]
        xn = sb("xn", [P, C])
        xcT = sb("xcT", [P, 4, P])
        q = [sb(f"q{k}", [P, C]) for k in range(2)]
        kk = [sb(f"kk{k}", [P, C]) for k in range(2)]
        prod = [sb(f"prod{k}", [P, HALF, C]) for k in range(2)]
        pv = [sb(f"pv{k}", [P, b_ - a_, C]) for k, (a_, b_) in enumerate(PVH)]
        vs = [sb(f"vs{k}", [P, C]) for k in range(2)]
        lg = sb("lg", [P, NH, NH])
        pr = sb("pr", [P, NH, NH])
        mx = sb("mx", [P, NH])
        sm = sb("sm", [P, NH])
        rsm = sb("rsm", [P, NH])
        ao = [sb(f"ao{k}", [P, NH, HD]) for k in range(2)]
        aoT = sb("aoT", [P, KC, P])
        x2T = sb("x2T", [P, KC, P])
        cat = [sb(f"cat{k}", [P, ROW]) for k in range(2)]
        junk = [sb(f"junk{k}", [P, C]) for k in range(2)]
        nm, nm16, va, ve, rs, nb = (sb(n, [P, 2]) for n in ("nm", "nm16", "va", "ve", "rs", "nb"))
        eps2 = sb("eps2", [P, 2])
        half2 = sb("half2", [P, 2])
        gm = sb("gm", [P, 1])
        ge = sb("ge", [P, NE])
        gs = sb("gs", [P, 1])
        glog = sb("glog", [P, NT, NE])

        def bank(name):
            return es.enter_context(nc.psum_tensor(name, [P, 512], f32))

        bT, bQ, bO, bA, bY, bG = (bank(n) for n in ("bT", "bQ", "bO", "bA", "bY", "bG"))
        bKV = [bank("bKV0"), bank("bKV1")]

        programs = {e: [] for e in ("sync", "gpsimd", "vector", "scalar", "tensor")}

        def on_engine(name):
            return programs[name].append

        def done(inst, ev, by=1):
            return inst.then_inc(sem(ev), by)

        def need(eng, ev, n):
            if not isinstance(n, int) or n > 0:
                eng.wait_ge(sem(ev), n)

        wst4 = sb("wst4", [P, 4, KC, C])
        wst = [wst4[:, w, :, :] for w in range(4)]
        NR = BW // P
        bst, bres, bres2 = (sb(n, [NR, P]) for n in ("bst", "bres", "bres2"))
        bsp = sb("bsp", [NR, 3, P], bf16)
        wrp = sb("wrp", [P, KC, P])
        wrT = sb("wrT", [P, KC, P])
        wgT = sb("wgT", [NG, NE])
        wgb = sb("wgb", [P, NE * NG])
        wgs = sb("wgs", [P, NE * NG])
        nr2, nrm, nri = (sb(n, [P, NE]) for n in ("nr2", "nrm", "nri"))
        warm = sb("warm", [P, 2])
        b1s = sb("b1s", [NE * KH, P])
        BIASES = ((bq, 0), (bk, C), (bv, 2 * C), (bd, 3 * C))

        def load_biases(eng, some):
            for src, o in some:
                done(eng.dma_start(bst[o // P:(o + C) // P, :], src.rearrange("(r c) -> r c", c=P)), "ld_b", 16)

        @on_engine("sync")
        def _(eng):
            load_biases(eng, BIASES[:2])
            done(eng.dma_start(xt[0][:, :], x[0]), "ld_x0", 16)
            for w, src in enumerate((Wq, Wk, Wv, Wd)):
                if w == 1:
                    done(eng.dma_start(ct[0][:, :], ctx_in[0]), "ld_c0", 16)
                done(eng.dma_start(wst[w], src.rearrange("(a p) c -> p a c", p=P)), f"ld_w{w}", 16)
            need(eng, "pad0", 1)
            done(eng.dma_start(wrp[:, :, 0:NG], w_red.rearrange("(a p) g -> p a g", p=P)), "ld_g", 16)
            done(eng.dma_start(wgb[:, :], wg.rearrange("e g -> (e g)").rearrange("(o n) -> o n", o=1)
                               .broadcast_to((P, NE * NG))), "ld_g", 16)
            with nc.allow_non_contiguous_dma("wg transposed, 128 elements"):
                done(eng.dma_start(wgT[:, :], wg.rearrange("e g -> g e")), "ld_g", 16)
            done(eng.dma_start(b1s[:, :], b1.rearrange("e (k p) -> (e k) p", p=P)), "ld_b1", 16)
            need(eng, "brow0", 1)
            need(eng, "bsplit", 1)
            done(eng.dma_start(bias_scr.rearrange("k (r c) -> r k c", c=P), bsp[:, :, :]), "st_b", 16)
            need(eng, "st_b", 16)
            done(eng.dma_start(brow[0:3, :], bias_scr), "ld_br", 16)

        @on_engine("scalar")
        def _(eng):
            load_biases(eng, BIASES[2:])
            need(eng, "filled", 1)
            eng.activation(warm[:, 0:1], half[:, :], ACT.Exp)

        @on_engine("gpsimd")
        def _(eng):
            eng.memset(ident[:, :], 0.0)
            eng.memset(half[:, :], -0.5)
            eng.memset(half2[:, :], -0.5)
            eng.memset(eps2[:, :], EPS)
            eng.memset(nm[:, :], 0.0)
            eng.memset(va[:, :], 0.0)
            eng.memset(ve[:, :], 1.0)
            eng.memset(tri[:, :], 0.0)
            done(eng.memset(seg[:, :, :], 1.0), "filled")
            need(eng, "filled", 1)
            done(eng.affine_select(out=ident[:, :], in_=ident[:, :], compare_op=ALU.not_equal, fill=1.0,
                                   base=0, pattern=[[-1, P]], channel_multiplier=1), "ident")
            done(eng.memset(wrp[:, :, :], 0.0), "pad0")
            done(eng.memset(brow[:, :], 0.0), "brow0")
            done(eng.memset(ones[:, :], 1.0), "ones")

        def constants(eng):
            for t, n in ((io_r1, P), (io_k1, NSP)):
                i_ = eng.iota(t[:, :], [[1, n]], base=0, channel_multiplier=0, allow_small_or_imprecise_dtypes=True)
            done(i_, "iotas")
            eng.affine_select(out=tri[:, :], in_=tri[:, :], compare_op=ALU.is_gt, fill=-1.0, base=0,
                              pattern=[[1, P]], channel_multiplier=-1)
            eng.memset(seg[:, :, 0:1], 0.0)
            eng.memset(one8[:, :], 1.0)
            for t, pattern, base, per in ((io_e[:, :, :], [[0, NT], [-1, NE]], NE, 0),
                                          (io_m[:, :, :], [[0, NE], [P, NT]], 0, 0),
                                          (io_n[:, :], [[1, NT]], 0, 0), (pid[:, :], [[0, 1]], 0, 1)):
                eng.iota(t, pattern, base=base, channel_multiplier=per, allow_small_or_imprecise_dtypes=True)
            done(eng.memset(half8[:, :], -0.5), "const")
            need(eng, "const", 1)
            need(eng, "nmax", 1)
            done(eng.tensor_tensor(nri[:, :], nrm[:, :], half8[:, :], ALU.pow), "gpow")

        def gate_parts(eng):
            need(eng, "wrt", 1)
            done(eng.tensor_copy(wrT[:, :, :], bY[:, 0:C].rearrange("p (a c) -> p a c", a=KC)), "wrTs")
            done(eng.tensor_copy(w1b[:, :, KC * HID:], bY[:, C:C + NE * KH].rearrange("p (e k) -> p e k", e=NE)),
                 "b1T")

        def fold_gate(eng):
            need(eng, "gpow", 1)
            need(eng, "gmm", 1)
            done(eng.tensor_tensor(gate[:, :, :], bG[:, 0:KC * NE].rearrange("p (a e) -> p a e", a=KC),
                                   nri[:, :].unsqueeze(1).broadcast_to((P, KC, NE)), ALU.mult), "gate")
            for k in range(2):
                done(eng.memset(cat[k][:, 2 * C:ROW], 0.0), "cat0")

        @on_engine("vector")
        def _(eng):
            need(eng, "ld_b", 16 * len(BIASES))
            done(eng.tensor_copy(bsp[:, 0, :], bst[:, :]), "bpart")
            need(eng, "bpart", 1)
            done(eng.tensor_tensor(bres[:, :], bst[:, :], bsp[:, 0, :], ALU.subtract), "bpart")
            need(eng, "bpart", 2)
            done(eng.tensor_copy(bsp[:, 1, :], bres[:, :]), "bpart")
            need(eng, "bpart", 3)
            done(eng.tensor_tensor(bres2[:, :], bres[:, :], bsp[:, 1, :], ALU.subtract), "bpart")
            need(eng, "bpart", 4)
            done(eng.tensor_copy(bsp[:, 2, :], bres2[:, :]), "bsplit")
            for w in range(4):
                need(eng, "wtr", w + 1)
                done(eng.tensor_copy(wT[:, :, w * C:(w + 1) * C],
                                     wbank[w][:, :].rearrange("p (a c) -> p a c", a=KC)), "wT")
            need(eng, "ld_g", 48)
            done(eng.tensor_tensor(wgs[:, :], wgb[:, :], wgb[:, :], ALU.mult), "gsq")
            need(eng, "gsq", 1)
            done(eng.tensor_reduce(nr2[:, :], wgs[:, :].rearrange("p (e g) -> p e g", e=NE), AX, ALU.add), "nr2")
            need(eng, "nr2", 1)
            done(eng.tensor_scalar(nrm[:, :], nr2[:, :], 1e-8, None, ALU.max), "nmax")
            need(eng, "iotas", 1)
            for wide, row, n in ((io_r, io_r1, P), (io_k, io_k1, NSP)):
                done(eng.tensor_copy(wide[:, :, :], row[:, :].unsqueeze(2).broadcast_to((P, n, NT // 2))), "wide")

        wbank = (bO, bKV[0], bKV[1], bA)

        def gate_transposes(eng):
            need(eng, "ld_g", 48)
            for a in range(KC):
                eng.transpose(bY[:, a * P:(a + 1) * P], wrp[:, a, :], ident[:, :])
            need(eng, "ld_b1", 16)
            done(eng.transpose(bY[:, C:C + NE * KH], b1s[:, :], ident[0:NE * KH, 0:NE * KH]), "wrt")

        def gate_products(eng):
            need(eng, "wrTs", 1)
            for a in range(KC):
                i_ = eng.matmul(bG[:, a * NE:(a + 1) * NE], wrT[0:NG, a, :], wgT[:, :], start=True, stop=True)
            done(i_, "gmm")

        @on_engine("tensor")
        def _(eng):
            need(eng, "ident", 1)
            for w in range(4):
                need(eng, f"ld_w{w}", 16)
                for a in range(KC):
                    for c in range(KC):
                        i_ = eng.transpose(wbank[w][:, c * C + a * P:c * C + (a + 1) * P],
                                           wst[w][:, a, c * P:(c + 1) * P], ident[:, :])
                done(i_, "wtr")
            need(eng, "wT", 4)

        LAGS, FIRST = 6, 8
        EXPERTS_IN = {0: (), 1: (0, 1), 2: (2, 3), 3: (4,), 4: (5,), 5: (6,), 6: (7,), 7: ()}

        def steps(eng, body, total, first, lags, unroll=2, lead=0):
            def step(i, c):
                def on(lag):
                    n = Tile(unroll, i, c - lag)
                    return n if i is not None or 0 <= c - lag < total else None
                body(on)
            last = first + (total - lead - first) // unroll * unroll
            for c in range(first):
                step(None, c)
            with eng.Fori(0, (last - first) // unroll) as i:
                for u in range(unroll):
                    step(i, first + u)
            for c in range(last, total + lags):
                step(None, c)

        @on_engine("sync")
        def _(eng):
            def experts(e):
                done(eng.dma_start(w1b[:, e, 0:KC * HID].rearrange("p (k h) -> p k h", k=KC),
                                   W1[e].rearrange("(k p) h -> p k h", p=P)), "ld_moe", 16)
                done(eng.dma_start(w2[:, e * KH * C:(e + 1) * KH * C].rearrange("p (k c) -> p k c", k=KH),
                                   W2[e].rearrange("(k p) c -> p k c", p=P)), "ld_moe", 16)

            def body(on):
                nxt, a, e, c, g = on(-1), on(0), on(3), on(4), on(6)
                if g:
                    need(eng, "score", g.at(1))
                    done(eng.dma_start(row_scr[bass.ds(g.at() * P, P), :], cat[g.par][:, :]),
                         f"st_r{g.par}", 16)
                if nxt:
                    need(eng, "xn", nxt.at(-1))
                    done(eng.dma_start(xt[nxt.par][:, :], x[nxt.at()]), f"ld_x{nxt.par}", 16)
                    need(eng, "tr_c", nxt.at(-1))
                    done(eng.dma_start(ct[nxt.par][:, :], ctx_in[nxt.at()]), f"ld_c{nxt.par}", 16)
                if c:
                    need(eng, "x2", c.at(-1))
                    done(eng.dma_start(xr[c.par][:, :], x[c.at()]), f"ld_xr{c.par}", 16)
                if e:
                    need(eng, "onorm", e.at(1))
                    done(eng.dma_start(attn_scr[e.at()].rearrange("i t d -> t i d"), ao[e.par][:, :, :]),
                         f"st_a{e.par}", 16)
                    need(eng, f"st_a{e.par}", e.turn(1) * 16)
                    need(eng, "tr_a", e.at(-1))
                    done(eng.dma_start(ar[e.par][:, :], attn_scr[e.at()]
                                       .rearrange("i (a b) d -> (i a) (b d)", b=NH)), f"ld_a{e.par}", 16)
                if a and a.i is None and a.c < FIRST:
                    for n in EXPERTS_IN[a.c]:
                        experts(n)
                    if a.c == FIRST - 1:
                        done(eng.dma_start(b2b[:, :], b2.rearrange("e c -> (e c)")
                                           .rearrange("(o n) -> o n", o=1).broadcast_to((P, NE * C))), "ld_moe", 16)
            steps(eng, body, NT, FIRST, LAGS, lead=1)
            for k in range(2):
                need(eng, f"st_r{k}", NT // 2 * 16)

        def on_dve(n):
            return n.i is None and n.c == 0

        def products(eng, n, h):
            if h == 0 or on_dve(n):
                need(eng, "kcp", n.at(1))
            need(eng, f"qkred{h}", n.at(0))
            done(eng.tensor_tensor(
                prod[h][:, :, :].rearrange("p i (j d) -> p i j d", j=NH),
                q[n.par][:, h * HALF * HD:(h + 1) * HALF * HD].rearrange("p (i d) -> p i d", d=HD)
                .unsqueeze(2).broadcast_to((P, HALF, NH, HD)),
                kk[n.par][:, :].rearrange("p (j d) -> p j d", d=HD)
                .unsqueeze(1).broadcast_to((P, HALF, NH, HD)), ALU.mult), f"qk{h}")

        ORDER = (1, 0, 2, PVG)

        def pv_mult(eng, b, g):
            lo, hi = PVH[g]
            need(eng, f"pvm{g}", b.at(0))
            done(eng.tensor_tensor(
                pv[g][:, :, :].rearrange("p j (i d) -> p j i d", i=NH),
                vs[b.par][:, lo * HD:hi * HD].rearrange("p (j d) -> p j d", d=HD)
                .unsqueeze(2).broadcast_to((P, hi - lo, NH, HD)),
                pr[:, :, lo:hi].rearrange("p i j -> p j i")
                .unsqueeze(3).broadcast_to((P, hi - lo, NH, HD)), ALU.mult),
                f"pvx{g}" if FOLD[g] else f"pv{g}")

        @on_engine("gpsimd")
        def _(eng):
            def body(on):
                a, d = on(0), on(5)
                if a or d:
                    turn = a.at(1) if a else d.at(6)
                    if a:
                        need(eng, "ve0", a.at(1))
                        need(eng, "xn", a.at(0))
                    if d:
                        need(eng, "ve1", d.at(1))
                        need(eng, "x2n", d.at(0))
                    done(eng.tensor_tensor(rs[:, :], ve[:, :], half2[:, :], ALU.pow), "rs")
                if a and a.i is None and a.c == 0:
                    constants(eng)
                v, b = on(1), on(2)
                if v:
                    products(eng, v, 0)
                if v and not on_dve(v):
                    products(eng, v, 1)
                if b:
                    need(eng, "vcp", b.at(1))
                    need(eng, "exp", b.at(1))
                    pv_mult(eng, b, PVG)
            steps(eng, body, NT, FIRST, LAGS)

        @on_engine("vector")
        def _(eng):
            def body(on):
                a, v, b, e, c, d, g = (on(k) for k in range(LAGS + 1))

                def fold(n, g):
                    k, m = FOLD[g], PVH[g][1] - PVH[g][0]
                    need(eng, f"pvx{g}", n.at(1))
                    done(eng.tensor_tensor(pv[g][:, 0:k, :], pv[g][:, 0:k, :], pv[g][:, m - k:m, :], ALU.add),
                         f"pv{g}")

                def qk_sum(h):
                    need(eng, f"qk{h}", b.at(1))
                    done(eng.tensor_reduce(lg[:, h * HALF:(h + 1) * HALF, :],
                                           prod[h][:, :, :].rearrange("p i (j d) -> p i j d", j=NH),
                                           AX, ALU.add), f"qkred{h}")

                if v and on_dve(v):
                    products(eng, v, 1)
                    gate_parts(eng)
                if b:
                    qk_sum(0)
                    qk_sum(1)
                if g:
                    need(eng, "gexp", g.at(1))
                    done(eng.reciprocal(cat[g.par][:, 2 * C:2 * C + 1], gs[:, :]), "score")
                if b:
                    need(eng, "qkred1", b.at(1))
                    done(eng.tensor_reduce(mx[:, :], lg[:, :, :], AX, ALU.max), "mx")
                if e:
                    need(eng, "sm", e.at(1))
                    need(eng, "onorm", e.at(0))
                    done(eng.reciprocal(rsm[:, :], sm[:, :]), "rsm")
                if b:
                    need(eng, "mx", b.at(1))
                    done(eng.tensor_tensor(lg[:, :, :], lg[:, :, :],
                                           mx[:, :].unsqueeze(2).broadcast_to((P, NH, NH)),
                                           ALU.subtract), "lsub")
                if e:
                    need(eng, f"pvm{ORDER[-1]}", e.at(1))
                    need(eng, f"st_a{e.par}", e.turn(0) * 16)
                    need(eng, "rsm", e.at(1))
                    done(eng.tensor_tensor(ao[e.par][:, :, :], bO[:, 0:C].rearrange("p (i d) -> p i d", i=NH),
                                           rsm[:, :].unsqueeze(2).broadcast_to((P, NH, HD)), ALU.mult), "onorm")
                if b:
                    need(eng, "vcp", b.at(1))
                    need(eng, "exp", b.at(1))
                    pv_mult(eng, b, 1)
                    need(eng, "rsm", b.at(0))
                    done(eng.tensor_reduce(sm[:, :], pr[:, :, :], AX, ALU.add), "sm")
                    pv_mult(eng, b, 0)
                if c:
                    need(eng, f"ld_xr{c.par}", c.turn(1) * 16)
                    need(eng, "wd", c.at(1))
                    need(eng, f"st_r{c.par}", c.turn(0) * 16)
                    done(eng.tensor_tensor(cat[c.par][:, C:2 * C], bY[:, 0:C], xr[c.par][:, :], ALU.add), "x2")
                if b:
                    fold(b, 0)
                if d:
                    need(eng, "glg", d.at(1))
                    done(eng.tensor_reduce(gm[:, :], bG[:, C:C + NE], AX, ALU.max), "gm")
                if b:
                    pv_mult(eng, b, 2)
                if d:
                    need(eng, "gm", d.at(1))
                    done(eng.tensor_scalar(glog[:, d.at(), :], bG[:, C:C + NE], gm[:, :], None,
                                           ALU.subtract), "gsub")
                if a and a.i is None and a.c == 4:
                    fold_gate(eng)
            steps(eng, body, NT, FIRST, LAGS)

        @on_engine("scalar")
        def _(eng):
            def moments(n, w, in_):
                need(eng, ("xn", "x2n")[w], n.at(0))
                done(eng.activation(junk[w][:, :], in_, ACT.Identity, scale=-1.0 / C, accum_out=nm[:, w:w + 1]),
                     f"nm{w}")
                need(eng, f"nm{w}", n.at(1))
                done(eng.activation(nm16[:, w:w + 1], nm[:, w:w + 1], ACT.Copy, scale=C ** -0.5), f"nms{w}")
                need(eng, f"nms{w}", n.at(1))
                done(eng.activation(junk[w][:, :], in_, ACT.Square, bias=nm16[:, w:w + 1], scale=C ** -0.5,
                                    accum_out=va[:, w:w + 1]), f"va{w}")
                need(eng, f"va{w}", n.at(1))
                done(eng.activation(ve[:, w:w + 1], va[:, w:w + 1], ACT.Identity, bias=eps2[:, w:w + 1]), f"ve{w}")

            def shift(n, w, turn):
                need(eng, "rs", turn)
                done(eng.activation(nb[:, w:w + 1], nm[:, w:w + 1], ACT.Copy, scale=rs[:, w:w + 1]), f"nb{w}")

            def normed(n, w, out_, in_, ev):
                need(eng, f"nb{w}", n.at(1))
                done(eng.activation(out_, in_, ACT.Identity, bias=nb[:, w:w + 1], scale=rs[:, w:w + 1]), ev)

            need(eng, "filled", 1)

            def front(n):
                need(eng, f"ld_x{n.par}", n.turn(1) * 16)
                moments(n, 0, xt[n.par][:, :])

            def body(on):
                a, v, b, c, d, g = (on(k) for k in (0, 1, 2, 4, 5, 6))
                if a and (a.i is not None or a.c == 0 or a.c >= FIRST):
                    front(a)
                if g:
                    need(eng, "gsub", g.at(1))
                    need(eng, "score", g.at(0))
                    done(eng.activation(ge[:, :], glog[:, g.at(), :], ACT.Exp, accum_out=gs[:, :]), "gexp")
                if d:
                    shift(d, 1, d.at(6))
                if a:
                    shift(a, 0, a.at(1))
                if d:
                    normed(d, 1, cat[d.par][:, 0:C], cat[d.par][:, C:2 * C], "x2n")
                if a:
                    need(eng, "tr_in", a.at(0))
                    normed(a, 0, xn[:, :], xt[a.par][:, :], "xn")
                if v:
                    need(eng, "kv", v.at(1))
                    need(eng, f"pv{PVD[-1]}", v.at(-1))
                    need(eng, f"pv{PVG}", v.at(-1))
                    done(eng.activation(vs[v.par][:, :], bKV[v.par][:, C:2 * C], ACT.Copy), "vcp")
                if c:
                    need(eng, "tr_a", c.at(1))
                    need(eng, "wd", c.at(0))
                    done(eng.activation(aoT[:, :, :], bA[:, 0:C].rearrange("p (a c) -> p a c", a=KC),
                                        ACT.Copy), "aoT")
                if d:
                    need(eng, "tr_g", d.at(1))
                    need(eng, "glg", d.at(0))
                    done(eng.activation(x2T[:, :, :], bG[:, 0:C].rearrange("p (a c) -> p a c", a=KC),
                                        ACT.Copy), "x2T")
                if b:
                    need(eng, "lsub", b.at(1))
                    need(eng, f"pv{PVD[-1]}", b.at(0))
                    need(eng, f"pv{PVG}", b.at(0))
                    done(eng.activation(pr[:, :, :], lg[:, :, :], ACT.Exp, scale=HD ** -0.5), "exp")
                if a:
                    need(eng, "tr_in", a.at(1))
                    need(eng, "kv", a.at(0))
                    done(eng.activation(xcT[:, :, :], bT[:, :].rearrange("p (a c) -> p a c", a=4),
                                        ACT.Copy), "xcT")
                    if a.i is None and a.c + 1 < FIRST:
                        front(Tile(a.unroll, None, a.c + 1))
                if a:
                    need(eng, "qq", a.at(1))
                    need(eng, "qk1", a.at(-1))
                    done(eng.activation(q[a.par][:, :], bQ[:, 0:C], ACT.Copy), "qcp")
                    need(eng, "kv", a.at(1))
                    done(eng.activation(kk[a.par][:, :], bKV[a.par][:, 0:C], ACT.Copy), "kcp")
                if c:
                    need(eng, "x2", c.at(1))
                    moments(c, 1, cat[c.par][:, C:2 * C])
            steps(eng, body, NT, FIRST, LAGS)
            eng.activation(warm[:, 1:2], half[:, :], ACT.Gelu)

        @on_engine("tensor")
        def _(eng):
            def bias(dst, off, n):
                return eng.matmul(dst, ones[:, :], brow[:, off:off + n], start=True, stop=False)

            def body(on):
                a, b, c, d = (on(k) for k in (0, 2, 4, 5))

                def pv_sum(g):
                    need(eng, f"pv{g}", b.at(1))
                    heads = PVH[g][1] - PVH[g][0] - FOLD[g]
                    for j in range(heads):
                        i_ = eng.matmul(bO[:, 0:C], ident[:, :], pv[g][:, j, :],
                                        start=(g == ORDER[0] and j == 0), stop=(g == ORDER[-1] and j == heads - 1))
                    done(i_, f"pvm{g}")

                if c:
                    need(eng, f"ld_a{c.par}", c.turn(1) * 16)
                    need(eng, "aoT", c.at(0))
                    for k in range(KC):
                        i_ = eng.transpose(bA[:, k * P:(k + 1) * P], ar[c.par][:, k * P:(k + 1) * P],
                                           ident[:, :])
                    done(i_, "tr_a")
                if a:
                    need(eng, f"ld_c{a.par}", a.turn(1) * 16)
                    need(eng, "xcT", a.at(0))
                    for k in range(KC):
                        i_ = eng.transpose(bT[:, (KC + k) * P:(KC + k + 1) * P],
                                           ct[a.par][:, k * P:(k + 1) * P], ident[:, :])
                    done(i_, "tr_c")
                if d:
                    need(eng, "x2n", d.at(1))
                    need(eng, "gsub", d.at(0))
                    if d.i is None and d.c == 0:
                        need(eng, "gate", 1)
                    for k in range(KC):
                        i_ = eng.transpose(bG[:, k * P:(k + 1) * P], cat[d.par][:, k * P:(k + 1) * P],
                                           ident[:, :])
                    done(i_, "tr_g")
                if a:
                    need(eng, "xn", a.at(1))
                    for k in range(KC):
                        i_ = eng.transpose(bT[:, k * P:(k + 1) * P], xn[:, k * P:(k + 1) * P], ident[:, :])
                    done(i_, "tr_in")
                if c:
                    need(eng, "x2", c.at(0))
                    if c.i is None and c.c == 0:
                        need(eng, "b1T", 1)
                    bias(bY[:, 0:C], 3 * C, C)
                if a:
                    need(eng, "qcp", a.at(0))
                    if a.i is None and a.c == 0:
                        need(eng, "ld_br", 16)
                        need(eng, "ones", 1)
                    bias(bQ[:, 0:C], 0, C)
                    need(eng, "vcp", a.at(-1))
                    need(eng, "kcp", a.at(-1))
                    bias(bKV[a.par][:, :], C, 2 * C)
                if c:
                    need(eng, "aoT", c.at(1))
                    for k in range(KC):
                        i_ = eng.matmul(bY[:, 0:C], aoT[:, k, :], wT[:, k, 3 * C:4 * C],
                                        start=False, stop=(k == KC - 1))
                    done(i_, "wd")
                if d:
                    need(eng, "x2T", d.at(1))
                    for k in range(KC):
                        i_ = eng.matmul(bG[:, C:C + NE], x2T[:, k, :], gate[:, k, :],
                                        start=(k == 0), stop=(k == KC - 1))
                    done(i_, "glg")
                if a:
                    need(eng, "xcT", a.at(1))
                    for k in range(KC):
                        i_ = eng.matmul(bQ[:, 0:C], xcT[:, k, :], wT[:, k, 0:C], start=False, stop=(k == KC - 1))
                    done(i_, "qq")
                    for k in range(KC):
                        i_ = eng.matmul(bKV[a.par][:, :], xcT[:, KC + k, :], wT[:, k, C:3 * C],
                                        start=False, stop=(k == KC - 1))
                    done(i_, "kv")
                    if a.i is None and a.c == 0:
                        gate_transposes(eng)
                    if a.i is None and a.c == 1:
                        gate_products(eng)
                if b:
                    need(eng, "onorm", b.at(0))
                    for g in ORDER:
                        pv_sum(g)
            steps(eng, body, NT, FIRST, LAGS)

        def fl(t):
            return t[:, :, :].rearrange("p a b -> p (a b)")

        r0, r1 = fl(prod[0]), fl(prod[1])
        oh = sb("oh", [P, NT, NE], bf16)
        idg = sb("idg", [P, NSP], i32)
        ids = sb("ids", [P, NSP], i32)
        texp = sb("texp", [P, NSP], i32)
        key = r0[:, 1024:1280].rearrange("p (n e) -> p n e", e=NE)
        top = r0[:, 1280:1280 + NT]
        inc = r0[:, 1568:1824].rearrange("p (e n) -> p e n", e=NE)
        til = r0[:, 1824:1824 + NE]
        tinc = r0[:, 1840:1840 + NE]
        texc = r0[:, 1856:1856 + NE]
        gtm = r1[:, 0:256].rearrange("p (e m) -> p e m", e=NE)
        exc = r1[:, 256:512].rearrange("p (e n) -> p e n", e=NE)
        slot = r1[:, 512:768].rearrange("p (e n) -> p e n", e=NE)
        ohe = oh[:, :, :].rearrange("p n e -> p e n")
        pos = r1[:, 768:800]
        posr = r1[:, 800:832].bitcast(bf16)[:, 0:NT]
        posk = r1[:, 832:864].bitcast(bf16)[:, 0:NT]
        pint = r1[:, 864:896].bitcast(i32)
        pir = r1[:, 896:928].bitcast(i32)
        pik = r1[:, 928:960].bitcast(i32)
        tcmp = r1[:, 960:960 + NSP * NE].rearrange("p (k e) -> p k e", e=NE)
        tsum = r1[:, 1280:1280 + NSP]
        tmin = r1[:, 1320:1320 + NSP]
        inv = r1[:, 1360:1360 + NSP]
        emp = r1[:, 1400:1400 + NSP]
        inv2 = r1[:, 1440:1440 + NSP]
        selr = [pv[k][:, 0:4, :].rearrange("p a b -> p (a b)").bitcast(bf16)
                .rearrange("p (r n) -> p r n", r=P) for k in range(2)]
        selk = [t.bitcast(bf16)[:, 0:16 * 3 * NSP].rearrange("p (w k n) -> p w k n", w=3, k=NSP)
                for t in (fl(pv[2]), w1s[0][:, 0:KC * HID])]

        @on_engine("vector")
        def _(eng):
            steps_ = [0]

            def then(i_):
                steps_[0] += 1
                done(i_, "rv")
                need(eng, "rv", steps_[0])

            need(eng, "const", 1)
            need(eng, "wide", 2)
            need(eng, "gsub", NT)
            then(eng.scalar_tensor_tensor(key, glog[:, :, :], 0.0, io_e[:, :, :], ALU.is_ge, ALU.mult))
            then(eng.tensor_reduce(top, key, AX, ALU.max))
            done(eng.tensor_tensor(oh[:, :, :], key, top.unsqueeze(2).broadcast_to((P, NT, NE)),
                                   ALU.is_equal), "oh")
            need(eng, "cnt", 1)
            then(eng.tensor_tensor_scan(inc.rearrange("p e n -> p (e n)"), seg[:, :, :].rearrange("p e n -> p (e n)"),
                                        bT[:, 0:NT * NE], 0.0, ALU.mult, ALU.add))
            then(eng.tensor_tensor(gtm, inc[:, :, NT - 1:NT].broadcast_to((P, NE, NT)), io_m[:, :, :], ALU.is_gt))
            then(eng.tensor_reduce(til, gtm, AX, ALU.add))
            then(eng.tensor_tensor_scan(tinc, one8[:, :], til, 0.0, ALU.mult, ALU.add))
            then(eng.tensor_tensor(texc, tinc, til, ALU.subtract))
            then(eng.scalar_tensor_tensor(exc, texc.unsqueeze(2).broadcast_to((P, NE, NT)), float(P), inc,
                                          ALU.mult, ALU.add))
            then(eng.tensor_tensor(slot, bQ[:, 0:NT * NE].rearrange("p (e n) -> p e n", e=NE), exc, ALU.add))
            then(eng.tensor_tensor(slot, slot, ohe, ALU.mult))
            then(eng.tensor_reduce(pos, slot.rearrange("p e n -> p n e"), AX, ALU.add))
            then(eng.tensor_copy(pint, pos))
            then(eng.tensor_scalar(pir, pint, P - 1, None, ALU.bitwise_and))
            then(eng.tensor_scalar(pik, pint, P.bit_length() - 1, None, ALU.logical_shift_right))
            then(eng.tensor_copy(posr, pir))
            then(eng.tensor_copy(posk, pik))
            NH2 = NT // 2
            for k in range(2):
                n = slice(k * NH2, (k + 1) * NH2)
                done(eng.tensor_tensor(selr[k], io_r[:, :, :], posr[:, n].unsqueeze(1).broadcast_to((P, P, NH2)),
                                       ALU.is_equal), "selr")
                then(eng.tensor_tensor(selk[k][:, 0, :, :], io_k[:, :, :],
                                       posk[:, n].unsqueeze(1).broadcast_to((P, NSP, NH2)), ALU.is_equal))
                done(eng.tensor_scalar(selk[k][:, 1, :, :], selk[k][:, 0, :, :], pid[:, :], None, ALU.mult), "selp")
                done(eng.tensor_tensor(selk[k][:, 2, :, :], selk[k][:, 0, :, :],
                                       io_n[:, n].unsqueeze(1).broadcast_to((P, NSP, NH2)), ALU.mult), "selk")
            then(eng.tensor_tensor(tcmp, tinc.unsqueeze(1).broadcast_to((P, NSP, NE)),
                                   io_k[:, :, 0:1].broadcast_to((P, NSP, NE)), ALU.is_le))
            then(eng.tensor_reduce(tsum, tcmp, AX, ALU.add))
            then(eng.tensor_scalar(tmin, tsum, float(NE - 1), None, ALU.min))
            done(eng.tensor_copy(texp[:, :], tmin), "texp")
            need(eng, "invmm", 1)
            then(eng.tensor_copy(inv2, bO[:, NSP:2 * NSP]))
            done(eng.scalar_tensor_tensor(idg[:, :], bO[:, 2 * NSP:3 * NSP], float(P), inv2, ALU.mult, ALU.add), "idg")
            then(eng.scalar_tensor_tensor(inv, bO[:, 2 * NSP:3 * NSP], float(P), inv2, ALU.mult, ALU.add))
            then(eng.tensor_scalar(emp, bO[:, 0:NSP], -float(NTOK), float(NTOK), ALU.mult, ALU.add))
            done(eng.tensor_tensor(ids[:, :], emp, inv, ALU.add), "ids")

        @on_engine("tensor")
        def _(eng):
            need(eng, "oh", 1)
            need(eng, "const", 1)
            need(eng, "xcT", NT)
            need(eng, "qcp", NT)
            need(eng, "onorm", NT)
            eng.matmul(bQ[:, 0:NT * NE], tri[:, :], ohe, start=True, stop=True)
            done(eng.matmul(bT[:, 0:NT * NE], ones[:, :], ohe, start=True, stop=True), "cnt")
            for n in range(NT):
                k = n // 16
                if n % 16 == 0:
                    need(eng, "selk", k + 1)
                i_ = eng.matmul(bO[:, 0:3 * NSP], selr[k][:, :, n % 16],
                                selk[k][:, :, :, n % 16].rearrange("p w k -> p (w k)"),
                                start=(n == 0), stop=(n == NT - 1))
            done(i_, "invmm")

        RB, FIRSTB, LAGSB = 4, 8, 4
        ig = [sb(f"ig{k}", [P, 1], i32) for k in range(RB)]
        isc = [sb(f"isc{k}", [P, 1], i32) for k in range(RB)]
        gr = [sb(f"gr{k}", [P, ROW]) for k in range(RB)]
        yo = [sb(f"yo{k}", [P, C]) for k in range(RB)]
        gT = [sb(f"gT{k}", [P, KC, P]) for k in range(2)]
        yb = [sb(f"yb{k}", [P, C]) for k in range(2)]
        hT = [sb(f"hT{k}", [P, KH, P]) for k in range(2)]
        held = sb("held", [P, 2])
        WARM = 11
        bH, bX, bYB = bKV, [bT, bQ], [bY, bG]

        @on_engine("gpsimd")
        def _(eng):
            def hold(k):
                eng.tensor_tensor(held[:, k:k + 1], half[:, :], half[:, :], ALU.add)

            need(eng, "idg", 1)
            for k in range(2):
                need(eng, f"st_r{k}", NT // 2 * 16)

            def body(on):
                a, c = on(0), on(4)
                if a:
                    k, at = a.slot(RB), eng.snap(a.at())
                    need(eng, f"gat{k}", a.turn(0, RB) * 16)
                    done(eng.tensor_copy(ig[k][:, :], idg[:, bass.ds(at, 1)]), "ig")
                if c:
                    if c.i is None and c.c == 0:
                        need(eng, "ids", 1)
                    k, at = c.slot(RB), eng.snap(c.at())
                    need(eng, f"sca{k}", c.turn(0, RB) * 16)
                    done(eng.tensor_copy(isc[k][:, :], ids[:, bass.ds(at, 1)]), "isc")
                if a:
                    k = a.slot(RB)
                    need(eng, "ig", a.at(1))
                    need(eng, "yo", a.at(1 - RB))
                    hold(0)
                    done(eng.indirect_dma_start(gr[k][:, :], None, row_scr,
                                                bass.IndirectOffsetOnAxis(ap=ig[k][:, :], axis=0)),
                         f"gat{k}", 16)
                if c:
                    k = c.slot(RB)
                    need(eng, "isc", c.at(1))
                    need(eng, "yo", c.at(1))
                    hold(1)
                    done(eng.indirect_dma_start(out, bass.IndirectOffsetOnAxis(ap=isc[k][:, :], axis=0),
                                                yo[k][:, :], None, bounds_check=NTOK - 1,
                                                oob_is_err=False), f"sca{k}", 16)
            steps(eng, body, NS, FIRSTB, LAGSB, RB)
            for k in range(RB):
                need(eng, f"sca{k}", len(range(k, NS, RB)) * 16)

        @on_engine("tensor")
        def _(eng):
            need(eng, "texp", 1)
            need(eng, "ids", 1)
            need(eng, "ld_moe", 16 * (2 * NE + 1))
            need(eng, "aoT", NT)
            for _ in range(WARM):
                eng.matmul(bA[:, :], ones[:, :], brow[:, 0:2 * C], start=True, stop=True)

            def body(on):
                x_, a, b = on(1), on(2), on(3)
                if b:
                    eb = eng.value_load(texp[0:1, bass.ds(b.at(), 1)], min_val=0, max_val=NE - 1)
                if a:
                    need(eng, "gel", a.at(-1))
                    need(eng, "w1s", a.at(1))
                    need(eng, "gT", a.at(1))
                    for k in range(KH):
                        for c in range(KC):
                            i_ = eng.matmul(bH[a.par][:, k * P:(k + 1) * P],
                                            w1s[a.par][:, c * HID + k * P:c * HID + (k + 1) * P],
                                            gT[a.par][:, c, :], start=(c == 0), stop=(c == KC - 1))
                    done(i_, "up")
                if x_:
                    need(eng, f"gat{x_.slot(RB)}", x_.turn(1, RB) * 16)
                    need(eng, "gT", x_.at(-1))
                    for k in range(KC):
                        i_ = eng.transpose(bX[x_.par][:, k * P:(k + 1) * P],
                                           gr[x_.slot(RB)][:, k * P:(k + 1) * P], ident[:, :])
                    done(i_, "gtr")
                if b:
                    need(eng, "yb", b.at(-1))
                    need(eng, "gel", b.at(1))
                    for k in range(KH):
                        i_ = eng.matmul(bYB[b.par][:, 0:C], hT[b.par][:, k, :],
                                        w2[:, bass.ds(eb * (KH * C) + k * C, C)],
                                        start=(k == 0), stop=(k == KH - 1))
                    done(i_, "down")
            steps(eng, body, NS, FIRSTB, LAGSB, RB)

        @on_engine("scalar")
        def _(eng):
            def body(on):
                a = on(2)
                if a:
                    need(eng, "up", a.at(1))
                    need(eng, "down", a.at(-1))
                    for k in range(KH):
                        i_ = eng.activation(hT[a.par][:, k, :], bH[a.par][:, k * P:(k + 1) * P], ACT.Gelu,
                                            bias=w1s[a.par][:, KC * HID + k:KC * HID + k + 1])
                    done(i_, "gel")
            steps(eng, body, NS, FIRSTB, LAGSB, RB)

        @on_engine("vector")
        def _(eng):
            need(eng, "texp", 1)
            need(eng, "ld_moe", 16 * (2 * NE + 1))

            def body(on):
                x_, b = on(1), on(3)
                if x_:
                    ex = eng.value_load(texp[0:1, bass.ds(x_.at(), 1)], min_val=0, max_val=NE - 1)
                    need(eng, "gel", x_.at(-1))
                    done(eng.tensor_scalar(w1s[x_.par][:, :], w1f[:, bass.ds(ex * W1W, W1W)], 1.0, None,
                                           ALU.mult), "w1s")
                    need(eng, "gtr", x_.at(1))
                    need(eng, "up", x_.at(-1))
                    done(eng.tensor_copy(gT[x_.par][:, :, :],
                                         bX[x_.par][:, 0:C].rearrange("p (a c) -> p a c", a=KC)), "gT")
                if b:
                    k = b.slot(RB)
                    eb = eng.value_load(texp[0:1, bass.ds(b.at(), 1)], min_val=0, max_val=NE - 1)
                    need(eng, "down", b.at(1))
                    done(eng.tensor_tensor(yb[b.par][:, :], bYB[b.par][:, 0:C], b2b[:, bass.ds(eb * C, C)],
                                           ALU.add), "yb")
                    need(eng, "yb", b.at(1))
                    need(eng, f"sca{k}", b.turn(0, RB) * 16)
                    done(eng.scalar_tensor_tensor(yo[k][:, :], yb[b.par][:, :], gr[k][:, 2 * C:2 * C + 1],
                                                  gr[k][:, C:2 * C], ALU.mult, ALU.add), "yo")
            steps(eng, body, NS, FIRSTB, LAGSB, RB)

        block = es.enter_context(nc.Block())
        for enter, parts in ((block.sync, programs["sync"]), (block.gpsimd, programs["gpsimd"]),
                             (block.vector, programs["vector"]), (block.scalar, programs["scalar"]),
                             (block.tensor, programs["tensor"])):
            enter(lambda eng, parts=parts: [part(eng) for part in parts])


_INS = ["x", "ctx_1024", "L0_xattn_Wq", "L0_xattn_bq", "L0_xattn_Wk", "L0_xattn_bk", "L0_xattn_Wv",
        "L0_xattn_bv", "L0_xattn_Wd", "L0_xattn_bd", "L0_ffn_w_red", "L0_ffn_wg", "L0_ffn_W1",
        "L0_ffn_b1", "L0_ffn_W2", "L0_ffn_b2"]


def kernel(**inputs):
    import numpy as np
    import concourse.bacc as bacc
    from concourse.bass_utils import run_bass_kernel_spmd

    nc = bacc.Bacc("TRN2", target_bir_lowering=False, num_devices=1)
    arrays, args = {}, []
    for name in _INS:
        a = np.ascontiguousarray(inputs[name])
        arrays[f"in_{name}"] = a
        args.append(nc.dram_tensor(f"in_{name}", a.shape, mybir.dt.from_np(a.dtype), kind="ExternalInput").ap())
    out = nc.dram_tensor("out", [NTOK, C], mybir.dt.float32, kind="ExternalOutput").ap()
    build(nc, *args, out)
    r = run_bass_kernel_spmd(nc, [arrays], core_ids=[0])
    return r.results[0]["out"].reshape(NT, P, C)
```
